# Optimizing a Trainium2 kernel written in Bass

```python
import numpy as np
import jax
import jax.numpy as jnp

def _softmax(x, axis=-1):
    return jax.nn.softmax(x, axis=axis)

def _gelu(x):
    return jax.nn.gelu(x, approximate=True)

def _silu(x):
    return jax.nn.silu(x)

def _sigmoid(x):
    return jax.nn.sigmoid(x)

def _layernorm(x, axis=-1, eps=1e-05):
    m = jnp.mean(x, axis=axis, keepdims=True)
    v = jnp.var(x, axis=axis, keepdims=True)
    return (x - m) / jnp.sqrt(v + eps)

def _scatter_add(tgt, idx, src, axis=0):
    return tgt.at[idx].add(src)

def _segment_sum(src, seg, n):
    return jax.ops.segment_sum(src, seg, n)
kernel_name = 'mk_cond_resid_d2_seqx_r2_584260'

def setup_inputs(seed: int=0):
    np.random.seed(seed)
    _w = jnp.asarray

    def _rec_inputs():
        import jax
        import jax.numpy as jnp
        _rk = jax.random.key(seed)
        x = -0.000125 + 0.9999 * jax.random.normal(jax.random.fold_in(_rk, 1), (2, 2048, 512), jnp.float32)
        _lenS = 2048 - jax.random.randint(jax.random.fold_in(_rk, 7), (2,), 0, max(1, 2048 // 4) + 1, jnp.int32)
        _lenS2 = 2048 - jax.random.randint(jax.random.fold_in(_rk, 8), (2,), 0, max(1, 2048 // 4) + 1, jnp.int32)
        cond_512 = 0.00782532 + 1.00527 * jax.random.normal(jax.random.fold_in(_rk, 11), (2, 256), jnp.float32)
        itok_BxS_0_999 = jax.random.randint(jax.random.fold_in(_rk, 12), (2, 2048), 0, 500, jnp.int32)
        itok_BxS_0_4 = jax.random.randint(jax.random.fold_in(_rk, 13), (2, 2048), 0, 5, jnp.int32)
        cond_64 = 0.0990542 + 1.04422 * jax.random.normal(jax.random.fold_in(_rk, 15), (2, 64), jnp.float32)
        fside_Bx32_0 = -0.136436 + 0.990155 * jax.random.normal(jax.random.fold_in(_rk, 16), (2, 32), jnp.float32)
        _validS = jnp.arange(2048)[None, :] < _lenS[:, None]
        _validS2 = jnp.arange(2048)[None, :] < _lenS2[:, None]
        _causal = jnp.tril(jnp.ones((2048, 2048), dtype=bool))
        mask_BxS_ik0 = jnp.where(jnp.broadcast_to(_validS[:, :], (2, 2048)), 0, 1).astype(jnp.int32)
        return (x, cond_512, itok_BxS_0_999, itok_BxS_0_4, cond_64, fside_Bx32_0, mask_BxS_ik0)
    x, cond_512, itok_BxS_0_999, itok_BxS_0_4, cond_64, fside_Bx32_0, mask_BxS_ik0 = _rec_inputs()

    def _L0_cond_setup():
        import jax, jax.numpy as jnp
        import numpy as np
        IN_DIM = 512
        OUT_DIM = 512
        MU_DIM = 256
        K = 30
        key = jax.random.key(seed)
        k1, k2, k3, k4, k5 = jax.random.split(key, 5)
        B, S = (16, 1024)
        x = jax.random.normal(k1, (B, S, IN_DIM), dtype=jnp.float32)
        mu = jax.random.normal(k2, (B, MU_DIM), dtype=jnp.float32)
        W_dec = jax.random.normal(k3, (MU_DIM, (IN_DIM + 1) * K), dtype=jnp.float32) / np.sqrt(MU_DIM)
        b_dec = jax.random.normal(k4, ((IN_DIM + 1) * K,), dtype=jnp.float32) * 0.01
        V = jax.random.normal(k5, (K, OUT_DIM), dtype=jnp.float32) / np.sqrt(K)
        return {'x': x, 'mu': mu, 'W_dec': W_dec, 'b_dec': b_dec, 'V': V}
    _L0_cond_all = _L0_cond_setup()
    _L0_cond_in = {k: v for k, v in _L0_cond_all.items() if k in ('W_dec', 'b_dec', 'V')}
    del _L0_cond_all

    def _L1_cond_setup():
        import jax, jax.numpy as jnp
        import numpy as np
        EPS = 1e-05

        def _ln(x, g, b):
            m = jnp.mean(x, axis=-1, keepdims=True)
            v = jnp.mean((x - m) ** 2, axis=-1, keepdims=True)
            return (x - m) * jax.lax.rsqrt(v + EPS) * g + b

        def _mlp_ln(s, W1, b1, W2, b2, g, b):
            h = jax.nn.silu(s @ W1 + b1) @ W2 + b2
            return _ln(h, g, b)
        key = jax.random.key(seed)
        B, S, D = (4, 1024, 512)
        MEM, NOI, RES = (256, 64, 32)
        ks = jax.random.split(key, 40)
        ki = iter(range(40))

        def nrm(shape, scale=0.02):
            return jax.random.normal(ks[next(ki)], shape, jnp.float32) * scale

        def gamma(shape):
            return jnp.ones(shape, jnp.float32) + nrm(shape)
        inp = {'x': jax.random.normal(ks[next(ki)], (B, S, D), jnp.float32), 'pathway_ids': jax.random.randint(ks[next(ki)], (B, S), 0, 500), 'compartment_ids': jax.random.randint(ks[next(ki)], (B, S), 0, 5), 'time_steps': jax.random.randint(ks[next(ki)], (B, S), 0, 5), 'scale_type': jax.random.randint(ks[next(ki)], (B, S), 0, 3), 'memory_state': jax.random.normal(ks[next(ki)], (B, MEM), jnp.float32), 'noise_state': jax.random.normal(ks[next(ki)], (B, NOI), jnp.float32), 'resource_state': jax.random.normal(ks[next(ki)], (B, RES), jnp.float32), 'pw_g': gamma((500, D)), 'pw_b': nrm((500, D)), 'cp_g': gamma((5, D)), 'cp_b': nrm((5, D)), 'tm_g': gamma((5, D)), 'tm_b': nrm((5, D)), 'ms_g': gamma((3, D)), 'ms_b': nrm((3, D)), 'mem_W1': nrm((MEM, D)), 'mem_b1': jnp.zeros((D,)), 'mem_W2': nrm((D, D)), 'mem_b2': jnp.zeros((D,)), 'mem_g': gamma((D,)), 'mem_be': jnp.zeros((D,)), 'noi_W1': nrm((NOI, D)), 'noi_b1': jnp.zeros((D,)), 'noi_W2': nrm((D, D)), 'noi_b2': jnp.zeros((D,)), 'noi_g': gamma((D,)), 'noi_be': jnp.zeros((D,)), 'res_W1': nrm((RES, D)), 'res_b1': jnp.zeros((D,)), 'res_W2': nrm((D, D)), 'res_b2': jnp.zeros((D,)), 'res_g': gamma((D,)), 'res_be': jnp.zeros((D,)), 'int_W1': nrm((6 * D, D)), 'int_b1': jnp.zeros((D,)), 'int_W2': nrm((D, D)), 'int_b2': jnp.zeros((D,)), 'int_g': gamma((D,)), 'int_be': jnp.zeros((D,)), 'aw': jnp.ones((6,), jnp.float32) / 6.0}
        return inp
    _L1_cond_all = _L1_cond_setup()
    _L1_cond_in = {k: v for k, v in _L1_cond_all.items() if k in ('pw_g', 'pw_b', 'cp_g', 'cp_b', 'tm_g', 'tm_b', 'ms_g', 'ms_b', 'mem_W1', 'mem_b1', 'mem_W2', 'mem_b2', 'mem_g', 'mem_be', 'noi_W1', 'noi_b1', 'noi_W2', 'noi_b2', 'noi_g', 'noi_be', 'res_W1', 'res_b1', 'res_W2', 'res_b2', 'res_g', 'res_be', 'int_W1', 'int_b1', 'int_W2', 'int_b2', 'int_g', 'int_be', 'aw')}
    del _L1_cond_all
    return {'x': x, 'cond_512': cond_512, 'itok_BxS_0_999': itok_BxS_0_999, 'itok_BxS_0_4': itok_BxS_0_4, 'cond_64': cond_64, 'fside_Bx32_0': fside_Bx32_0, 'mask_BxS_ik0': mask_BxS_ik0, 'L0_cond_W_dec': _L0_cond_in['W_dec'], 'L0_cond_b_dec': _L0_cond_in['b_dec'], 'L0_cond_V': _L0_cond_in['V'], 'L1_cond_pw_g': _L1_cond_in['pw_g'], 'L1_cond_pw_b': _L1_cond_in['pw_b'], 'L1_cond_cp_g': _L1_cond_in['cp_g'], 'L1_cond_cp_b': _L1_cond_in['cp_b'], 'L1_cond_tm_g': _L1_cond_in['tm_g'], 'L1_cond_tm_b': _L1_cond_in['tm_b'], 'L1_cond_ms_g': _L1_cond_in['ms_g'], 'L1_cond_ms_b': _L1_cond_in['ms_b'], 'L1_cond_mem_W1': _L1_cond_in['mem_W1'], 'L1_cond_mem_b1': _L1_cond_in['mem_b1'], 'L1_cond_mem_W2': _L1_cond_in['mem_W2'], 'L1_cond_mem_b2': _L1_cond_in['mem_b2'], 'L1_cond_mem_g': _L1_cond_in['mem_g'], 'L1_cond_mem_be': _L1_cond_in['mem_be'], 'L1_cond_noi_W1': _L1_cond_in['noi_W1'], 'L1_cond_noi_b1': _L1_cond_in['noi_b1'], 'L1_cond_noi_W2': _L1_cond_in['noi_W2'], 'L1_cond_noi_b2': _L1_cond_in['noi_b2'], 'L1_cond_noi_g': _L1_cond_in['noi_g'], 'L1_cond_noi_be': _L1_cond_in['noi_be'], 'L1_cond_res_W1': _L1_cond_in['res_W1'], 'L1_cond_res_b1': _L1_cond_in['res_b1'], 'L1_cond_res_W2': _L1_cond_in['res_W2'], 'L1_cond_res_b2': _L1_cond_in['res_b2'], 'L1_cond_res_g': _L1_cond_in['res_g'], 'L1_cond_res_be': _L1_cond_in['res_be'], 'L1_cond_int_W1': _L1_cond_in['int_W1'], 'L1_cond_int_b1': _L1_cond_in['int_b1'], 'L1_cond_int_W2': _L1_cond_in['int_W2'], 'L1_cond_int_b2': _L1_cond_in['int_b2'], 'L1_cond_int_g': _L1_cond_in['int_g'], 'L1_cond_int_be': _L1_cond_in['int_be'], 'L1_cond_aw': _L1_cond_in['aw']}

def reference(x, cond_512, itok_BxS_0_999, itok_BxS_0_4, cond_64, fside_Bx32_0, mask_BxS_ik0, L0_cond_W_dec, L0_cond_b_dec, L0_cond_V, L1_cond_pw_g, L1_cond_pw_b, L1_cond_cp_g, L1_cond_cp_b, L1_cond_tm_g, L1_cond_tm_b, L1_cond_ms_g, L1_cond_ms_b, L1_cond_mem_W1, L1_cond_mem_b1, L1_cond_mem_W2, L1_cond_mem_b2, L1_cond_mem_g, L1_cond_mem_be, L1_cond_noi_W1, L1_cond_noi_b1, L1_cond_noi_W2, L1_cond_noi_b2, L1_cond_noi_g, L1_cond_noi_be, L1_cond_res_W1, L1_cond_res_b1, L1_cond_res_W2, L1_cond_res_b2, L1_cond_res_g, L1_cond_res_be, L1_cond_int_W1, L1_cond_int_b1, L1_cond_int_W2, L1_cond_int_b2, L1_cond_int_g, L1_cond_int_be, L1_cond_aw):
    import jax
    import jax.numpy as jnp

    def _L0_cond_ref(x, mu, W_dec, b_dec, V):
        import jax, jax.numpy as jnp
        import numpy as np
        IN_DIM = 512
        OUT_DIM = 512
        MU_DIM = 256
        K = 30
        B = mu.shape[0]
        U = (mu @ W_dec + b_dec).reshape(B, IN_DIM + 1, K)
        param = jnp.einsum('bik,kj->bij', U, V)
        weight = param[:, :-1, :]
        bias = param[:, -1, :]
        out = jnp.einsum('bsd,bde->bse', x, weight)
        out = out + bias[:, None, :]
        return out

    def _L1_cond_ref(x, pathway_ids, compartment_ids, time_steps, scale_type, memory_state, noise_state, resource_state, pw_g, pw_b, cp_g, cp_b, tm_g, tm_b, ms_g, ms_b, mem_W1, mem_b1, mem_W2, mem_b2, mem_g, mem_be, noi_W1, noi_b1, noi_W2, noi_b2, noi_g, noi_be, res_W1, res_b1, res_W2, res_b2, res_g, res_be, int_W1, int_b1, int_W2, int_b2, int_g, int_be, aw):
        import jax, jax.numpy as jnp
        import numpy as np
        EPS = 1e-05

        def _ln(x, g, b):
            m = jnp.mean(x, axis=-1, keepdims=True)
            v = jnp.mean((x - m) ** 2, axis=-1, keepdims=True)
            return (x - m) * jax.lax.rsqrt(v + EPS) * g + b

        def _mlp_ln(s, W1, b1, W2, b2, g, b):
            h = jax.nn.silu(s @ W1 + b1) @ W2 + b2
            return _ln(h, g, b)
        h = _ln(x, pw_g[pathway_ids], pw_b[pathway_ids])
        h = _ln(h, cp_g[compartment_ids], cp_b[compartment_ids])
        t = _ln(x, tm_g[time_steps], tm_b[time_steps])
        m = x + _mlp_ln(memory_state, mem_W1, mem_b1, mem_W2, mem_b2, mem_g, mem_be)[:, None, :]
        n = x + _mlp_ln(noise_state, noi_W1, noi_b1, noi_W2, noi_b2, noi_g, noi_be)[:, None, :]
        r = x + _mlp_ln(resource_state, res_W1, res_b1, res_W2, res_b2, res_g, res_be)[:, None, :]
        s = _ln(x, ms_g[scale_type], ms_b[scale_type])
        w = jax.nn.softmax(aw)
        cat = jnp.concatenate([w[0] * h, w[1] * t, w[2] * m, w[3] * n, w[4] * r, w[5] * s], axis=-1)
        return _mlp_ln(cat, int_W1, int_b1, int_W2, int_b2, int_g, int_be)
    x = x + _L0_cond_ref(x, cond_512, L0_cond_W_dec, L0_cond_b_dec, L0_cond_V)
    x = x + _L1_cond_ref(x, itok_BxS_0_999, itok_BxS_0_4, itok_BxS_0_4, mask_BxS_ik0, cond_512, cond_64, fside_Bx32_0, L1_cond_pw_g, L1_cond_pw_b, L1_cond_cp_g, L1_cond_cp_b, L1_cond_tm_g, L1_cond_tm_b, L1_cond_ms_g, L1_cond_ms_b, L1_cond_mem_W1, L1_cond_mem_b1, L1_cond_mem_W2, L1_cond_mem_b2, L1_cond_mem_g, L1_cond_mem_be, L1_cond_noi_W1, L1_cond_noi_b1, L1_cond_noi_W2, L1_cond_noi_b2, L1_cond_noi_g, L1_cond_noi_be, L1_cond_res_W1, L1_cond_res_b1, L1_cond_res_W2, L1_cond_res_b2, L1_cond_res_g, L1_cond_res_be, L1_cond_int_W1, L1_cond_int_b1, L1_cond_int_W2, L1_cond_int_b2, L1_cond_int_g, L1_cond_int_be, L1_cond_aw)
    return x

_drawn_inputs = setup_inputs


def setup_inputs(seed=0):
    import zlib

    import numpy as np

    out = dict(_drawn_inputs(seed))
    spreads = {'L1_cond_mem_b1': (0.0, 2.0),
     'L1_cond_mem_b2': (0.0, 2.0),
     'L1_cond_mem_be': (0.0, 2.0),
     'L1_cond_noi_b1': (0.0, 2.0),
     'L1_cond_noi_b2': (0.0, 2.0),
     'L1_cond_noi_be': (0.0, 2.0),
     'L1_cond_res_b1': (0.0, 2.0),
     'L1_cond_res_b2': (0.0, 2.0),
     'L1_cond_res_be': (0.0, 2.0),
     'L1_cond_int_b1': (0.0, 0.8),
     'L1_cond_int_b2': (0.0, 0.8),
     'L1_cond_int_be': (0.0, 0.8),
     'L1_cond_aw': (0.1666666716337204, 0.6)}
    factors = {'cond_64': 8.0,
     'fside_Bx32_0': 8.0,
     'L0_cond_b_dec': 5.79,
     'L1_cond_pw_g': 64.0,
     'L1_cond_pw_b': 64.0,
     'L1_cond_cp_g': 64.0,
     'L1_cond_cp_b': 64.0,
     'L1_cond_tm_g': 64.0,
     'L1_cond_tm_b': 64.0,
     'L1_cond_ms_g': 64.0,
     'L1_cond_ms_b': 64.0,
     'L1_cond_mem_W1': 8.0,
     'L1_cond_mem_W2': 8.0,
     'L1_cond_mem_g': 64.0,
     'L1_cond_noi_W1': 8.0,
     'L1_cond_noi_W2': 8.0,
     'L1_cond_noi_g': 64.0,
     'L1_cond_res_W1': 8.0,
     'L1_cond_res_W2': 8.0,
     'L1_cond_res_g': 64.0,
     'L1_cond_int_g': 64.0}
    for name, (base, spread) in spreads.items():
        noise = np.random.default_rng([zlib.crc32(name.encode()), seed]).standard_normal(out[name].shape)
        drawn = base * np.exp(spread * noise) if base else spread * noise
        out[name] = jnp.asarray(drawn.astype(out[name].dtype))
    for name, factor in factors.items():
        out[name] = (out[name] * factor).astype(out[name].dtype)
    return out
```

```python
from contextlib import ExitStack

import numpy as np
import concourse.bass as bass
from concourse import mybir

F32 = mybir.dt.float32
F32R = mybir.dt.float32r
I32 = mybir.dt.int32
ALU = mybir.AluOpType
ACT = mybir.ActivationFunctionType
AX = mybir.AxisListType

B, S, D = 2, 2048, 512
MU, NOI, RES = 256, 64, 32
RANK = 30
P = 128
KC = D // P
Q = 32
TILES = B * S // P
EPS = 1e-5
DECW = P * RANK
X, T_, S_, H = range(4)
HI, LO = 0, 1
WH, WT, WM, WN, WR, WS = range(6)
FIRST, LAST = 3, TILES - 3


class Tile:

    def __init__(self, s, i=None):
        self.s, self.i, self.slot, self.batch = s, i, s % 2, s % 2

    def plus(self, k):
        return Tile(self.s + k, self.i)

    def count(self, each=1, extra=1):
        v = (self.s + extra) * each
        return v if self.i is None else self.i * (2 * each) + v

    def slot_count(self, each):
        v = (self.s // 2 + 1) * each
        return v if self.i is None else self.i * each + v

    def pair(self):
        return self.s // 2 if self.i is None else self.i + self.s // 2

    def exists(self):
        return self.i is not None or 0 <= self.s < TILES


def steps(eng, emit):
    for n in range(-2, FIRST):
        emit(Tile(n))
    with eng.Fori(0, (LAST - FIRST) // 2) as i:
        emit(Tile(FIRST, i))
        emit(Tile(FIRST + 1, i))
    for n in range(LAST, TILES + 1):
        emit(Tile(n))


def build(nc, d, out):
    with ExitStack() as ctx:
        def sb(name, shape, dt=F32, c=ctx):
            return c.enter_context(nc.sbuf_tensor(name, shape, dt))

        W1 = sb("W1", [P, 4, 2, KC, D], F32R)
        W2 = sb("W2", [P, 2, KC, D], F32R)
        Ust = sb("Ust", [P, B, KC, P], F32R)
        Vst = sb("Vst", [P, D], F32R)
        VWst = sb("VWst", [P, D], F32R)
        BT = sb("BT", [P, D], F32R)
        ub = sb("ub", [P, B])
        ident = sb("ident", [P, P + 1])
        kept = dict(W1=W1, W2=W2, Ust=Ust, Vst=Vst, VWst=VWst, BT=BT, ub=ub, ident=ident)
        prepare(nc, d, kept)
        tiles(nc, d, out, kept)


def prepare(nc, d, k):
    W1, W2, Ust, Vst, VWst, BT, ub = k["W1"], k["W2"], k["Ust"], k["Vst"], k["VWst"], k["BT"], k["ub"]
    NSTAGE = 3
    MLP_W1, MLP_W2, INT_W2, DEC = 0, 1, 4, 5
    with ExitStack() as ctx:
        def sb(name, shape, dt=F32):
            return ctx.enter_context(nc.sbuf_tensor(name, shape, dt))

        def pb(name, shape):
            return ctx.enter_context(nc.psum_tensor(name, shape, F32))

        def sem(name):
            return ctx.enter_context(nc.semaphore(name))

        raw = sb("raw", [P, 6, KC, D])
        stage = sb("stage", [P, NSTAGE, DECW])
        LM = sb("LM", [P, 3, KC, P])
        BL = sb("BL", [P, 3, KC, P])
        Wx = sb("Wx", [P, D])
        st = sb("st", [P, MU // P + 2, B])
        sv = sb("sv", [P, 4, 3, KC])
        bdec = sb("bdec", [P, KC, RANK])
        wlast = sb("wlast", [P, 2, P])
        ubc = sb("ubc", [P, 3])
        aw = sb("aw", [P, 6])
        wexp = sb("wexp", [P, 6])
        wsm = sb("wsm", [P, 6])
        sc = sb("sc", [P, 4])
        ones = sb("ones", [P, P])
        selr = sb("selr", [1, P + D])
        hid = sb("hid", [P, 3, KC, B])
        vec = sb("vec", [P, 3, KC, B])
        sq = sb("sq", [P, 3, KC, B])
        mean = sb("mean", [P, 3, B])
        var = sb("var", [P, 3, B])
        rst = sb("rst", [P, 3, B])
        mhalf = sb("mhalf", [P, 3 * B])
        Uf = sb("Uf", [P, KC, RANK, B])

        pU = pb("pU", [P, KC, 2, Q, B])
        pL = pb("pL", [P, 512])
        pM1 = pb("pM1", [P, 512])
        pM2 = pb("pM2", [P, 512])
        pS1 = pb("pS1", [P, 512])
        pS2 = pb("pS2", [P, 512])
        pVW = pb("pVW", [P, D])
        pBT = pb("pBT", [P, D])

        small_in = sem("small_in")
        raw_in = [sem(f"raw_in{i}") for i in range(6)]
        stage_in = [sem(f"stage_in{i}") for i in range(NSTAGE)]
        stage_used = sem("stage_used")
        int_w2_used = sem("int_w2_used")
        dve = sem("dve_prep")
        max_ready = sem("max_ready")
        exp_ready = sem("exp_ready")
        w_ready = sem("w_ready")
        scaled = sem("scaled")
        pre_ready = sem("pre_ready")
        hid_ready = sem("hid_ready")
        vec_ready = sem("vec_ready")
        sum_ready = sem("sum_ready")
        sq_ready = sem("sq_ready")
        sqsum_ready = sem("sqsum_ready")
        var_ready = sem("var_ready")
        rst_ready = sem("rst_ready")
        pool_prep = sem("pool_prep")
        lm_ready = sem("lm_ready")
        ust_zero = sem("ust_zero")
        w2_hi = sem("w2_hi")
        w1_hi = sem("w1_hi")
        ulast_ready = sem("ulast_ready")
        bt_ready = sem("bt_ready")
        vw_ready = sem("vw_ready")
        ones_ready = sem("ones_ready")

        smalls = [
            (k["ident"][:, :], d["consts"][:, 0:P + 1]), (ubc[:, :], d["ubc"]),
            (selr[0:1, 0:P], d["selrow"]), (selr[0:1, P:P + D], d["int_b1"]),
            (st[:, 0:MU // P, :], d["memT"].rearrange("(c p) b -> p c b", p=P)),
            (st[0:NOI, MU // P, :], d["noiT"]), (st[0:RES, MU // P + 1, :], d["resT"]),
            (sv[:, :, :, :], d["sv"].rearrange("p (a m f) -> p a m f", a=4, m=3)),
            (aw[:, :], d["aw"].to_broadcast([P, 6])),
            (bdec[:, :, :], d["bdec"].rearrange("(c p) r -> p c r", p=P)),
            (wlast[:, :, :], d["wlast"].rearrange("(c p) r -> p c r", p=P)),
            (LM[:, 0, :, :], d["VT4"]),
            (LM[:, 1, :, :], d["VT4"]),
            (LM[:, 2, :, :], d["VT4"]),
            (BL[:, :, :, :], d["BL"]),
            (Wx[:, :], d["V4"]),
        ]
        SMALLS = 16 * len(smalls)
        mlp_w1 = [(d["mem_W1"], MU // P, P), (d["noi_W1"], 1, NOI), (d["res_W1"], 1, RES)]
        DMAS = [3] + [1] * 4 + [1] * (2 * KC)
        STAGED = [16 * sum(DMAS[i % NSTAGE:i + 1:NSTAGE]) for i in range(len(DMAS))]

        def stage_view(item, width=D, n=KC):
            return stage[:, item % NSTAGE, 0:n * width].rearrange("p (c n) -> p c n", n=width)

        block = ctx.enter_context(nc.Block())

        @block.scalar
        def _(act):
            for dst, src in smalls:
                act.dma_start(dst, src).then_inc(small_in, 16)
            act.wait_ge(max_ready, 1)
            nc.scalar.activation(wexp[:, :], aw[:, :], ACT.Exp, bias=sc[:, 0:1],
                                 accum_out=sc[:, 1:2]).then_inc(exp_ready, 1)
            act.wait_ge(w_ready, 1)
            for blk in (WN, WR, WS):
                act.wait_ge(raw_in[blk], 16)
                nc.scalar.activation(raw[:, blk, :, :], raw[:, blk, :, :], ACT.Copy,
                                     scale=wsm[:, blk:blk + 1]).then_inc(scaled, 1)
            act.wait_ge(pre_ready, 1)
            nc.scalar.activation(hid[:, :, :, :], hid[:, :, :, :], ACT.Silu, bias=0.0).then_inc(hid_ready, 1)
            act.wait_ge(stage_in[INT_W2 % NSTAGE], STAGED[INT_W2])
            nc.scalar.activation(W2[:, HI, :, :], stage_view(INT_W2), ACT.Copy).then_inc(w2_hi, 1)
            act.wait_ge(scaled, 6)
            for blk, src in ((T_, WT), (S_, WS), (H, WH)):
                nc.scalar.activation(W1[:, blk, HI, :, :], raw[:, src, :, :], ACT.Copy).then_inc(w1_hi, 1)

        @block.sync
        def _(sp):
            for i, (src, n, rows) in enumerate(mlp_w1):
                sp.dma_start(stage[0:rows, 0, i * 2 * D:i * 2 * D + n * D].rearrange("p (c n) -> p c n", n=D),
                             src.rearrange("(c p) n -> p c n", p=rows)).then_inc(stage_in[0], 16)
            for m, name in enumerate(("mem_W2", "noi_W2", "res_W2", "int_W2")):
                item = MLP_W2 + m
                if item >= NSTAGE:
                    sp.wait_ge(stage_used, item - NSTAGE + 1)
                sp.dma_start(stage_view(item), d[name].rearrange("(c p) n -> p c n", p=P)) \
                  .then_inc(stage_in[item % NSTAGE], 16)
                if m < 3:
                    for blk in (2 * m, 2 * m + 1):
                        sp.dma_start(raw[:, blk, :, :],
                                     d["int_W1"][blk * D:(blk + 1) * D, :].rearrange("(c p) n -> p c n", p=P)) \
                          .then_inc(raw_in[blk], 16)
            for c in range(KC):
                for m in range(2):
                    item = DEC + 2 * c + m
                    if item - NSTAGE == INT_W2:
                        sp.wait_ge(int_w2_used, 1)
                    else:
                        sp.wait_ge(stage_used, item - NSTAGE + 1 - (1 if item - NSTAGE > INT_W2 else 0))
                    sp.dma_start(stage[:, item % NSTAGE, :], d["W_dec"][m * P:(m + 1) * P, c * DECW:(c + 1) * DECW]) \
                      .then_inc(stage_in[item % NSTAGE], 16)

        @block.tensor
        def _(pe):
            pe.wait_ge(small_in, SMALLS)
            pe.wait_ge(ones_ready, 1)
            for m in range(2):
                last = nc.tensor.matmul(pL[:, 0:B], wlast[:, m, :], st[:, m, :], start=(m == 0), stop=(m == 1))
            last.then_inc(ulast_ready, 1)
            pe.wait_ge(stage_in[0], STAGED[0])
            for m, (_, n, rows) in enumerate(mlp_w1):
                w = stage[0:rows, 0, m * 2 * D:m * 2 * D + n * D].rearrange("p (c n) -> p c n", n=D)
                for f in range(KC):
                    col = (m * KC + f) * B
                    for c in range(n):
                        last = nc.tensor.matmul(pM1[:, col:col + B], w[:, c, f * P:(f + 1) * P],
                                                st[0:rows, (c if m == 0 else MU // P + m - 1), :],
                                                start=(c == 0), stop=(c == n - 1))
            last.then_inc(stage_used, 1)
            pe.wait_ge(hid_ready, 1)
            for m in range(3):
                pe.wait_ge(stage_in[(MLP_W2 + m) % NSTAGE], STAGED[MLP_W2 + m])
                w = stage_view(MLP_W2 + m)
                for f in range(KC):
                    col = (m * KC + f) * B
                    for c in range(KC):
                        last = nc.tensor.matmul(pM2[:, col:col + B], w[:, c, f * P:(f + 1) * P], hid[:, m, c, :],
                                                start=(c == 0), stop=(c == KC - 1))
                last.then_inc(stage_used, 1)
            pe.wait_ge(vec_ready, 1)
            nc.tensor.matmul(pS1[:, 0:3 * KC * B], ones[:, :], vec[:, :, :, :].rearrange("p m f b -> p (m f b)"),
                             start=True, stop=True).then_inc(sum_ready, 1)
            pe.wait_ge(sq_ready, 1)
            nc.tensor.matmul(pS2[:, 0:3 * KC * B], ones[:, :], sq[:, :, :, :].rearrange("p m f b -> p (m f b)"),
                             start=True, stop=True).then_inc(sqsum_ready, 1)
            pe.wait_ge(scaled, 6)
            n = 0
            for t, blk in enumerate((WH, WT, WS)):
                for c in range(KC):
                    last = nc.tensor.matmul(pBT[:, :], BL[:, t, c, :], raw[:, blk, c, :],
                                            start=(n == 0), stop=(n == 3 * KC - 1))
                    n += 1
            last.then_inc(bt_ready, 1)
            pe.wait_ge(lm_ready, 1)
            nc.tensor.matmul(pVW[:, :], selr[0:1, 0:P], selr[0:1, P:P + D], start=True, stop=False)
            for m, blk in enumerate((WM, WN, WR)):
                for c in range(KC):
                    last = nc.tensor.matmul(pVW[:, :], LM[:, m, c, :], raw[:, blk, c, :],
                                            start=False, stop=(m == 2 and c == KC - 1))
            last.then_inc(vw_ready, 1)
            for c in range(KC):
                for m in range(2):
                    item = DEC + 2 * c + m
                    pe.wait_ge(stage_in[item % NSTAGE], STAGED[item])
                    w = stage[:, item % NSTAGE, :].rearrange("p (i r) -> p r i", r=RANK)
                    for r in range(RANK):
                        last = nc.tensor.matmul(pU[:, c, m, r, :], w[:, r, :], st[:, m, :], start=True, stop=True)
                    last.then_inc(stage_used, 1)

        @block.gpsimd
        def _(pool):
            nc.gpsimd.memset(ones[:, :], 1.0).then_inc(ones_ready, 1)
            nc.gpsimd.memset(mhalf[:, :], -0.5).then_inc(pool_prep, 1)
            nc.gpsimd.memset(Ust[:, :, :, :].bitcast(F32), 0.0).then_inc(ust_zero, 1)
            pool.wait_ge(pool_prep, 1)
            pool.wait_ge(var_ready, 1)
            nc.gpsimd.tensor_tensor(rst[:, :, :].rearrange("p m b -> p (m b)"),
                                    var[:, :, :].rearrange("p m b -> p (m b)"), mhalf[:, :],
                                    ALU.pow).then_inc(rst_ready, 1)
            for n, (blk, src) in enumerate(((T_, WT), (S_, WS))):
                pool.wait_ge(w1_hi, n + 1)
                nc.gpsimd.tensor_tensor(W1[:, blk, LO, :, :], raw[:, src, :, :], W1[:, blk, HI, :, :].bitcast(F32),
                                        ALU.subtract)

        @block.vector
        def _(v):
            seen = [0]

            def link(ins):
                seen[0] += 1
                ins.then_inc(dve, 1)
                v.wait_ge(dve, seen[0])

            v.wait_ge(small_in, SMALLS)
            nc.vector.tensor_reduce(sc[:, 0:1], aw[:, :], axis=AX.X, op=ALU.max, negate=True).then_inc(max_ready, 1)
            v.wait_ge(exp_ready, 1)
            link(nc.vector.reciprocal(sc[:, 2:3], sc[:, 1:2]))
            nc.vector.tensor_scalar(wsm[:, :], wexp[:, :], sc[:, 2:3], None, ALU.mult).then_inc(w_ready, 1)
            v.wait_ge(stage_used, MLP_W1 + 1)
            pm1 = pM1[:, 0:3 * KC * B].rearrange("p (m f b) -> p m f b", m=3, b=B)
            for b in range(B):
                last = nc.vector.tensor_tensor(hid[:, :, :, b], pm1[:, :, :, b], sv[:, 0, :, :], ALU.add)
            last.then_inc(pre_ready, 1)
            link(nc.vector.tensor_copy(Vst[:, :], Wx[:, :]))
            nc.vector.tensor_tensor(Vst[3 * Q:P, :], Wx[3 * Q:P, :], Vst[3 * Q:P, :].bitcast(F32), ALU.subtract)
            v.wait_ge(ulast_ready, 1)
            nc.vector.scalar_tensor_tensor(out=ub[:, :], in0=pL[:, 0:B], scalar=ubc[:, 0:1], in1=ubc[:, 1:3],
                                           op0=ALU.add, op1=ALU.add)
            v.wait_ge(w_ready, 1)
            for blk in (WH, WT, WM):
                v.wait_ge(raw_in[blk], 16)
                nc.vector.tensor_scalar(raw[:, blk, :, :], raw[:, blk, :, :], wsm[:, blk:blk + 1], None,
                                        ALU.mult).then_inc(scaled, 1)
            v.wait_ge(stage_used, MLP_W2 + 3)
            pm2 = pM2[:, 0:3 * KC * B].rearrange("p (m f b) -> p m f b", m=3, b=B)
            for b in range(B):
                last = nc.vector.tensor_tensor(vec[:, :, :, b], pm2[:, :, :, b], sv[:, 1, :, :], ALU.add)
            last.then_inc(vec_ready, 1)
            v.wait_ge(sum_ready, 1)
            link(nc.vector.tensor_reduce(mean[:, :, :],
                                         pS1[:, 0:3 * KC * B].rearrange("p (m f b) -> p m b f", m=3, b=B),
                                         axis=AX.X, op=ALU.add))
            link(nc.vector.tensor_scalar(mean[:, :, :], mean[:, :, :], 1.0 / D, None, ALU.mult))
            for f in range(KC):
                last = nc.vector.tensor_tensor(vec[:, :, f, :], vec[:, :, f, :], mean[:, :, :], ALU.subtract)
            link(last)
            nc.vector.tensor_tensor(sq[:, :, :, :], vec[:, :, :, :], vec[:, :, :, :], ALU.mult).then_inc(sq_ready, 1)
            v.wait_ge(sqsum_ready, 1)
            link(nc.vector.tensor_reduce(var[:, :, :],
                                         pS2[:, 0:3 * KC * B].rearrange("p (m f b) -> p m b f", m=3, b=B),
                                         axis=AX.X, op=ALU.add))
            nc.vector.tensor_scalar(var[:, :, :], var[:, :, :], 1.0 / D, EPS, ALU.mult, ALU.add).then_inc(var_ready, 1)
            v.wait_ge(rst_ready, 1)
            for f in range(KC):
                last = nc.vector.tensor_tensor(vec[:, :, f, :], vec[:, :, f, :], rst[:, :, :], ALU.mult)
            link(last)
            for b in range(B):
                last = nc.vector.tensor_tensor(vec[:, :, :, b], vec[:, :, :, b], sv[:, 2, :, :], ALU.mult)
            link(last)
            for b in range(B):
                last = nc.vector.tensor_tensor(vec[:, :, :, b], vec[:, :, :, b], sv[:, 3, :, :], ALU.add)
            link(last)
            for col in (RANK, 3 * Q + RANK):
                last = nc.vector.tensor_copy(LM[:, :, :, col:col + B], vec[:, :, :, :])
            last.then_inc(lm_ready, 1)
            v.wait_ge(w2_hi, 1)
            nc.vector.tensor_tensor(W2[:, LO, :, :], stage_view(INT_W2), W2[:, HI, :, :].bitcast(F32),
                                    ALU.subtract).then_inc(int_w2_used, 1)
            v.wait_ge(scaled, 6)
            for c in range(KC):
                link(nc.vector.tensor_tensor(Wx[:, :], raw[:, WM, c, :], raw[:, WN, c, :], ALU.add))
                link(nc.vector.tensor_tensor(Wx[:, :], Wx[:, :], raw[:, WR, c, :], ALU.add))
                link(nc.vector.tensor_copy(W1[:, X, HI, c, :], Wx[:, :]))
                link(nc.vector.tensor_tensor(W1[:, X, LO, c, :], Wx[:, :], W1[:, X, HI, c, :].bitcast(F32),
                                             ALU.subtract))
            v.wait_ge(bt_ready, 1)
            link(nc.vector.tensor_copy(BT[:, :], pBT[:, :]))
            for q in (1, 3):
                last = nc.vector.tensor_tensor(BT[q * Q:(q + 1) * Q, :], pBT[q * Q:(q + 1) * Q, :],
                                               BT[q * Q:(q + 1) * Q, :].bitcast(F32), ALU.subtract)
            link(last)
            v.wait_ge(vw_ready, 1)
            link(nc.vector.tensor_copy(VWst[:, :], pVW[:, :]))
            link(nc.vector.tensor_tensor(VWst[3 * Q:P, :], pVW[3 * Q:P, :], VWst[3 * Q:P, :].bitcast(F32),
                                         ALU.subtract))
            v.wait_ge(w1_hi, 3)
            nc.vector.tensor_tensor(W1[:, H, LO, :, :], raw[:, WH, :, :], W1[:, H, HI, :, :].bitcast(F32),
                                    ALU.subtract)
            v.wait_ge(stage_used, 4 + 2 * KC)
            v.wait_ge(ust_zero, 1)
            for b in range(B):
                last = nc.vector.tensor_tensor(Uf[:, :, :, b], pU[:, :, 0, 0:RANK, b], bdec[:, :, :], ALU.add)
            link(last)
            link(nc.vector.tensor_tensor(Uf[:, :, :, :], Uf[:, :, :, :], pU[:, :, 1, 0:RANK, :], ALU.add))
            for b in range(B):
                for q in (0, 2, 3):
                    last = nc.vector.tensor_copy(Ust[:, b, :, q * Q:q * Q + RANK], Uf[:, :, :, b])
            link(last)
            for b in range(B):
                last = nc.vector.tensor_tensor(Ust[:, b, :, Q:Q + RANK], Uf[:, :, :, b],
                                               Ust[:, b, :, 0:RANK].bitcast(F32), ALU.subtract)
            link(last)


def tiles(nc, d, out, k):
    W1, W2, Ust, Vst, VWst, BT, ub = k["W1"], k["W2"], k["Ust"], k["Vst"], k["VWst"], k["BT"], k["ub"]
    ident, inquad = k["ident"][:, 0:P], k["ident"][:, P:P + 1]
    with ExitStack() as ctx:
        def sb(name, shape, dt=F32):
            return ctx.enter_context(nc.sbuf_tensor(name, shape, dt))

        def pb(name, shape):
            return ctx.enter_context(nc.psum_tensor(name, shape, F32))

        def sem(name):
            return ctx.enter_context(nc.semaphore(name))

        def sem2(name):
            return [sem(f"{name}{i}") for i in range(2)]

        b2bc, gbc, bebc = (sb(name, [P, D]) for name in ("b2bc", "gbc", "bebc"))
        xT = sb("xT", [P, 2, KC, P])
        xop = sb("xop", [P, 2, 2, KC, P], F32R)
        x0 = sb("x0", [P, 2, D])
        idx = sb("idx", [P, 2, 3], I32)
        idxrep = sb("idxrep", [P, 2, P], I32)
        OH = sb("OH", [P, 2, P], F32R)
        stack = sb("stack", [P, 2, P], F32R)
        x1 = sb("x1", [P, 2, D])
        xb = sb("xb", [P, 2, D])
        xhat = sb("xhat", [P, 2, D])
        pwt = sb("pwt", [P, 2, 2 * D])
        ctt = sb("ctt", [P, 2, 2 * D])
        sgt = sb("sgt", [P, 2, D])
        tt = sb("tt", [P, D])
        st = sb("st_", [P, D])
        h1 = sb("h1", [P, D])
        hn = sb("hn", [P, D])
        ht = sb("ht", [P, D])
        ops = sb("ops", [P, 3, 2, KC, P], F32R)
        z = sb("z", [P, D])
        zop = sb("zop", [P, 2, KC, P], F32R)
        o = sb("o", [P, D])
        u = sb("u", [P, D])
        y = sb("y", [P, 2, D])
        bn = sb("bn", [P, 3, 6])
        mv = sb("mv", [P, 3, 2])
        ve = sb("ve", [P, 3])
        rs = sb("rs", [P, 3])
        mhalf = sb("mhalf_", [P, 1])
        warm = sb("warm", [P, 1])

        HID = [pb(f"HID{i}", [P, D]) for i in range(2)]
        OUT = [pb(f"OUT{i}", [P, D]) for i in range(2)]
        TP = [pb(f"TP{i}", [P, D]) for i in range(2)]
        XU = pb("XU", [P, 512])
        XV = pb("XV", [P, D])

        xT_in, x0_in, idx_in, rep_in = sem2("xT_in"), sem2("x0_in"), sem2("idx_in"), sem2("rep_in")
        pw_in, ct_in, sg_in, stored = sem2("pw_in"), sem2("ct_in"), sem2("sg_in"), sem2("stored")
        x_hi, x_lo, x_used, oh_ready = sem("x_hi"), sem("x_lo"), sem("x_used"), sem("oh_ready")
        xu_ready, stack_part, stack_ready, xv_ready = sem("xu_ready"), sem("stack_part"), sem("stack_ready"), sem("xv_ready")
        x1_ready, bn_done, mv1_ready, r1_ready = sem("x1_ready"), sem("bn_done"), sem("mv1_ready"), sem("r1_ready")
        xhat_ready, t_ready, s_ready, h1_part, h1_ready = (sem("xhat_ready"), sem("t_ready"), sem("s_ready"),
                                                           sem("h1_part"), sem("h1_ready"))
        mv2_ready, r2_ready, hn_ready, h_ready = sem("mv2_ready"), sem("r2_ready"), sem("hn_ready"), sem("h_ready")
        tT, sT, hT, zT = sem("tT"), sem("sT"), sem("hT"), sem("zT")
        t_hi, s_hi, h_hi, z_hi = sem("t_hi"), sem("s_hi"), sem("h_hi"), sem("z_hi")
        t_lo, s_lo, h_lo, z_lo = sem("t_lo"), sem("s_lo"), sem("h_lo"), sem("z_lo")
        hid_ready, z_ready, w2_done, o_ready = sem("hid_done"), sem("z_ready"), sem("w2_done"), sem("o_ready")
        mv3_ready, r3_ready, xb_ready, u_ready, y_ready = (sem("mv3_ready"), sem("r3_ready"), sem("xb_ready"),
                                                           sem("u_done"), sem("y_ready"))
        pool_part, mhalf_ready = sem("pool_part"), sem("mhalf_ready")
        rows_in = sem("rows_in")
        block = ctx.enter_context(nc.Block())

        outv = out.rearrange("b (j p) n -> b j p n", p=P)

        @block.sync
        def _(sp):
            def step(n):
                a = n.plus(2)
                if a.exists():
                    s, old = a.slot, a.plus(-2)
                    if old.exists():
                        sp.wait_ge(x_lo, old.count())
                    sp.dma_start(xT[:, s, :, :], d["xT"][s, bass.ds(a.pair(), 1), :, :, :].rearrange(
                        "o p c t -> (o p) c t")).then_inc(xT_in[s], 16)
                    if old.exists():
                        sp.wait_ge(x1_ready, old.count())
                    sp.dma_start(x0[:, s, :], d["x"][s, bass.ds(a.pair(), 1), :, :].rearrange("o p n -> (o p) n")) \
                      .then_inc(x0_in[s], 16)
                    if old.exists():
                        sp.wait_ge(sg_in[s], old.slot_count(16))
                        sp.wait_ge(ct_in[s], old.slot_count(16))
                        sp.wait_ge(pw_in[s], old.slot_count(16))
                    sp.dma_start(idx[:, s, :], d["idx"][s, bass.ds(a.pair(), 1), :, :].rearrange("o p n -> (o p) n")) \
                      .then_inc(idx_in[s], 16)
                    if old.exists():
                        sp.wait_ge(oh_ready, old.count())
                    for half in range(2):
                        sp.dma_start(idxrep[half * P // 2:(half + 1) * P // 2, s, :],
                                     d["rows"][s, half, bass.ds(a.pair(), 1), :].to_broadcast([P // 2, P])) \
                          .then_inc(rep_in[s], 16)
                c = n.plus(-1)
                if c.exists():
                    sp.wait_ge(y_ready, c.count())
                    sp.dma_start(outv[c.batch, bass.ds(c.pair(), 1), :, :].rearrange("o p n -> (o p) n"),
                                 y[:, c.slot, :]).then_inc(stored[c.slot], 16)

            steps(sp, step)
            for s in range(2):
                sp.wait_ge(stored[s], 16 * TILES // 2)

        @block.gpsimd
        def _(pool):
            nc.gpsimd.memset(mhalf[:, :], -0.5).then_inc(mhalf_ready, 1)

            def rstd(which, t, have, done):
                pool.wait_ge(have, t.count())
                pool.nop(nofuse=True)
                nc.gpsimd.tensor_scalar(ve[:, which:which + 1], mv[:, which, 1:2], EPS, 1.0, ALU.add, ALU.mult) \
                    .then_inc(pool_part, 1)
                parts[0] += 1
                pool.wait_ge(pool_part, part_count(t))
                nc.gpsimd.tensor_tensor(rs[:, which:which + 1], ve[:, which:which + 1], mhalf[:, :],
                                        ALU.pow).then_inc(done, 1)

            parts = [0]
            base = [0, None]

            def part_count(t):
                return parts[0] if base[1] is None else base[1] * base[0] + parts[0]

            def step(n):
                a, f, c = n.plus(2), n.plus(1), n.plus(-1)
                if a.exists():
                    s, old = a.slot, a.plus(-2)
                    pool.wait_ge(idx_in[s], a.slot_count(16))
                    if old.exists():
                        pool.wait_ge(h_ready, old.count())
                    pool.nop(nofuse=True)
                    for dst, table, col, got in ((ctt[:, s, :], d["ct"], 1, ct_in), (sgt[:, s, :], d["ms_g"], 2, sg_in),
                                                 (pwt[:, s, :], d["pw"], 0, pw_in)):
                        pool.indirect_dma_start(out=dst, out_offset=None, in_=table,
                                                in_offset=bass.IndirectOffsetOnAxis(ap=idx[:, s, col:col + 1], axis=0)) \
                            .then_inc(got[s], 16)
                if f.exists():
                    s = f.slot
                    rstd(0, f, mv1_ready, r1_ready)
                    pool.wait_ge(xhat_ready, f.count())
                    pool.wait_ge(pw_in[s], f.slot_count(16))
                    if f.plus(-1).exists():
                        pool.wait_ge(hn_ready, f.count(extra=0))
                    nc.gpsimd.tensor_tensor(h1[:, :], xhat[:, s, :], pwt[:, s, 0:D], ALU.mult).then_inc(h1_part, 1)
                    pool.wait_ge(h1_part, f.count())
                    nc.gpsimd.tensor_tensor(h1[:, :], h1[:, :], pwt[:, s, D:2 * D], ALU.add).then_inc(h1_ready, 1)
                if a.exists():
                    s = a.slot
                    pool.wait_ge(x_hi, a.count())
                    nc.gpsimd.tensor_tensor(xop[:, s, LO, :, :], xT[:, s, :, :], xop[:, s, HI, :, :].bitcast(F32),
                                            ALU.subtract).then_inc(x_lo, 1)
                if f.exists():
                    rstd(1, f, mv2_ready, r2_ready)
                if c.exists():
                    rstd(2, c, mv3_ready, r3_ready)
                if f.exists():
                    s = f.slot
                    if f.plus(-2).exists():
                        pool.wait_ge(y_ready, f.count(extra=-1))
                    pool.wait_ge(x1_ready, f.count())
                    nc.gpsimd.tensor_tensor(xb[:, s, :], x1[:, s, :], bebc[:, :], ALU.add).then_inc(xb_ready, 1)

            pool.wait_ge(mhalf_ready, 1)
            pool.wait_ge(rows_in, 48)
            for n in range(-2, FIRST):
                step(Tile(n))
            with pool.Fori(0, (LAST - FIRST) // 2) as i:
                before = parts[0]
                base[:] = [6, i]
                step(Tile(FIRST, i))
                step(Tile(FIRST + 1, i))
                assert parts[0] - before == 6
            parts[0] = before + 6 * ((LAST - FIRST) // 2)
            base[1] = None
            for n in range(LAST, TILES + 1):
                step(Tile(n))

        @block.scalar
        def _(act):
            for row, name in ((bebc, "int_be"), (b2bc, "int_b2"), (gbc, "int_g")):
                act.dma_start(row[:, :], d[name].to_broadcast([P, D])).then_inc(rows_in, 16)
            nc.scalar.activation(warm[:, :], ident[:, 0:1], ACT.Silu, bias=0.0)

            def split_hi(dst, bank, have, t, done):
                act.wait_ge(have, t.count())
                nc.scalar.activation(dst.rearrange("p c t -> p (c t)"), bank[:, :], ACT.Copy).then_inc(done, 1)

            def step(n):
                a, m, c = n.plus(2), n, n.plus(-1)
                if m.exists():
                    split_hi(ops[:, 0, HI, :, :], TP[0], tT, m, t_hi)
                    split_hi(ops[:, 1, HI, :, :], TP[1], sT, m, s_hi)
                if a.exists():
                    s, old = a.slot, a.plus(-2)
                    act.wait_ge(xT_in[s], a.slot_count(16))
                    if old.exists():
                        act.wait_ge(x_used, old.count())
                    nc.scalar.activation(xop[:, s, HI, :, :], xT[:, s, :, :], ACT.Copy).then_inc(x_hi, 1)
                if c.exists():
                    split_hi(zop[:, HI, :, :], TP[0], zT, c, z_hi)
                if m.exists():
                    split_hi(ops[:, 2, HI, :, :], TP[1], hT, m, h_hi)
                    act.wait_ge(hid_ready, m.count())
                    nc.scalar.activation(z[:, :], HID[m.slot][:, :], ACT.Silu, bias=0.0).then_inc(z_ready, 1)

            steps(act, step)

        @block.vector
        def _(v):
            def split_lo(dst, hi, bank, have, t, done):
                v.wait_ge(have, t.count())
                nc.vector.tensor_tensor(dst.rearrange("p c t -> p (c t)"), bank[:, :],
                                        hi.bitcast(F32).rearrange("p c t -> p (c t)"), ALU.subtract).then_inc(done, 1)

            def stats(which, src, t, before, ready):
                nc.vector.bn_stats(bn[:, which, :], src).then_inc(bn_done, 1)
                parts[0] += 1
                v.wait_ge(bn_done, parts[0] if base[1] is None else base[1] * base[0] + parts[0])
                v.nop(nofuse=True)
                nc.vector.bn_aggr(mv[:, which, :], bn[:, which, :]).then_inc(ready, 1)

            parts = [0]
            base = [0, None]

            def step(n):
                a, f, m, c = n.plus(2), n.plus(1), n, n.plus(-1)
                if m.exists():
                    split_lo(ops[:, 0, LO, :, :], ops[:, 0, HI, :, :], TP[0], t_hi, m, t_lo)
                    split_lo(ops[:, 1, LO, :, :], ops[:, 1, HI, :, :], TP[1], s_hi, m, s_lo)
                if f.exists():
                    s, bias = f.slot, ub[:, f.batch:f.batch + 1]
                    v.wait_ge(xu_ready, f.count())
                    if f.plus(-2).exists():
                        v.wait_ge(x_used, f.count(extra=-1))
                    nc.vector.tensor_scalar(stack[:, s, :], XU[:, 0:P], bias, None, ALU.add).then_inc(stack_part, 1)
                    v.wait_ge(stack_part, f.count())
                    nc.vector.scalar_tensor_tensor(out=stack[2 * Q:3 * Q, s, :], in0=XU[2 * Q:3 * Q, 0:P],
                                                   scalar=bias[2 * Q:3 * Q, :], in1=stack[2 * Q:3 * Q, s, :].bitcast(F32),
                                                   op0=ALU.add, op1=ALU.subtract).then_inc(stack_ready, 1)
                if a.exists():
                    s = a.slot
                    v.wait_ge(rep_in[s], a.slot_count(32))
                    if m.exists():
                        v.wait_ge(x_used, m.count())
                    nc.vector.tensor_scalar(OH[:, s, :], idxrep[:, s, :], inquad, None, ALU.is_equal).then_inc(oh_ready, 1)
                if f.exists():
                    s = f.slot
                    v.wait_ge(xv_ready, f.count())
                    v.wait_ge(x0_in[s], f.slot_count(16))
                    if f.plus(-2).exists():
                        v.wait_ge(xb_ready, f.count(extra=-1))
                    nc.vector.tensor_tensor(x1[:, s, :], XV[:, :], x0[:, s, :], ALU.add).then_inc(x1_ready, 1)
                    v.wait_ge(x1_ready, f.count())
                    stats(0, x1[:, s, :], f, 0, mv1_ready)
                if c.exists():
                    split_lo(zop[:, LO, :, :], zop[:, HI, :, :], TP[0], z_hi, c, z_lo)
                if f.exists():
                    s = f.slot
                    v.wait_ge(r1_ready, f.count())
                    if f.plus(-2).exists():
                        v.wait_ge(h1_part, f.count(extra=-1))
                    nc.vector.tensor_scalar(xhat[:, s, :], x1[:, s, :], mv[:, 0, 0:1], rs[:, 0:1],
                                            ALU.subtract, ALU.mult).then_inc(xhat_ready, 1)
                    v.wait_ge(xhat_ready, f.count())
                    v.wait_ge(ct_in[s], f.slot_count(16))
                    if m.exists():
                        v.wait_ge(tT, m.count())
                    nc.vector.tensor_tensor(tt[:, :], xhat[:, s, :], ctt[:, s, D:2 * D], ALU.mult).then_inc(t_ready, 1)
                    v.wait_ge(sg_in[s], f.slot_count(16))
                    if m.exists():
                        v.wait_ge(sT, m.count())
                    nc.vector.tensor_tensor(st[:, :], xhat[:, s, :], sgt[:, s, :], ALU.mult).then_inc(s_ready, 1)
                if m.exists():
                    split_lo(ops[:, 2, LO, :, :], ops[:, 2, HI, :, :], TP[1], h_hi, m, h_lo)
                if f.exists():
                    v.wait_ge(h1_ready, f.count())
                    stats(1, h1[:, :], f, 0, mv2_ready)
                if c.exists():
                    v.wait_ge(w2_done, c.count())
                    nc.vector.tensor_tensor(o[:, :], OUT[c.slot][:, :], b2bc[:, :], ALU.add).then_inc(o_ready, 1)
                    v.wait_ge(o_ready, c.count())
                    stats(2, o[:, :], c, 0, mv3_ready)
                if f.exists():
                    v.wait_ge(r2_ready, f.count())
                    nc.vector.tensor_scalar(hn[:, :], h1[:, :], mv[:, 1, 0:1], rs[:, 1:2],
                                            ALU.subtract, ALU.mult).then_inc(hn_ready, 1)
                if c.exists():
                    v.wait_ge(mv3_ready, c.count())
                    nc.vector.scalar_tensor_tensor(out=u[:, :], in0=o[:, :], scalar=mv[:, 2, 0:1], in1=gbc[:, :],
                                                   op0=ALU.subtract, op1=ALU.mult).then_inc(u_ready, 1)
                if f.exists():
                    v.wait_ge(hn_ready, f.count())
                    nc.vector.tensor_tensor(ht[:, :], hn[:, :], ctt[:, f.slot, 0:D], ALU.mult).then_inc(h_ready, 1)
                if c.exists():
                    s = c.slot
                    v.wait_ge(u_ready, c.count())
                    v.wait_ge(r3_ready, c.count())
                    v.wait_ge(xb_ready, c.count())
                    if c.plus(-2).exists():
                        v.wait_ge(stored[s], c.plus(-2).slot_count(16))
                    nc.vector.scalar_tensor_tensor(out=y[:, s, :], in0=u[:, :], scalar=rs[:, 2:3], in1=xb[:, s, :],
                                                   op0=ALU.mult, op1=ALU.add).then_inc(y_ready, 1)

            v.wait_ge(rows_in, 48)
            for n in range(-2, FIRST):
                step(Tile(n))
            with v.Fori(0, (LAST - FIRST) // 2) as i:
                before = parts[0]
                base[:] = [6, i]
                step(Tile(FIRST, i))
                step(Tile(FIRST + 1, i))
                assert parts[0] - before == 6
            parts[0] = before + 6 * ((LAST - FIRST) // 2)
            base[1] = None
            for n in range(LAST, TILES + 1):
                step(Tile(n))

        @block.tensor
        def _(pe):
            def transpose(dst, src, done):
                for c in range(KC):
                    last = nc.tensor.transpose(dst[:, c * P:(c + 1) * P], src[:, c * P:(c + 1) * P], ident)
                last.then_inc(done, 1)

            def product(bank, op, w, start, stop):
                for c in range(KC):
                    nc.tensor.matmul(bank[:, :], op[:, HI, c, :], w[:, HI, c, :], start=start and c == 0, stop=False)
                    nc.tensor.matmul(bank[:, :], op[:, HI, c, :], w[:, LO, c, :], start=False, stop=False)
                    last = nc.tensor.matmul(bank[:, :], op[:, LO, c, :], w[:, HI, c, :], start=False,
                                            stop=stop and c == KC - 1)
                return last

            def step(n):
                f, m, c = n.plus(1), n, n.plus(-1)
                if m.exists():
                    pe.wait_ge(t_ready, m.count())
                    if m.plus(-2).exists():
                        pe.wait_ge(z_lo, m.count(extra=-1))
                    transpose(TP[0], tt, tT)
                    pe.wait_ge(s_ready, m.count())
                    if m.plus(-1).exists():
                        pe.wait_ge(h_lo, m.count(extra=0))
                    transpose(TP[1], st, sT)
                if f.exists():
                    pe.wait_ge(x_lo, f.count())
                    if m.exists():
                        pe.wait_ge(stack_ready, m.count())
                    for q in range(KC):
                        for part in (HI, LO):
                            last = nc.tensor.matmul(XU[:, 0:P], Ust[:, f.batch, q, :], xop[:, f.slot, part, q, :],
                                                    start=(q == 0 and part == HI), stop=(q == KC - 1 and part == LO))
                    last.then_inc(xu_ready, 1)
                if m.exists():
                    if m.plus(-2).exists():
                        pe.wait_ge(z_ready, m.count(extra=-1))
                    product(HID[m.slot], xop[:, m.slot, :, :, :], W1[:, X, :, :, :], True, False)
                    nc.tensor.matmul(HID[m.slot][:, :], stack[:, m.slot, :], VWst[:, :], start=False, stop=False)
                    pe.wait_ge(oh_ready, m.count())
                    nc.tensor.matmul(HID[m.slot][:, :], OH[:, m.slot, :], BT[:, :], start=False, stop=False) \
                        .then_inc(x_used, 1)
                if f.exists():
                    pe.wait_ge(stack_ready, f.count())
                    if m.exists():
                        pe.wait_ge(x1_ready, m.count())
                    nc.tensor.matmul(XV[:, :], stack[:, f.slot, :], Vst[:, :], start=True, stop=True) \
                        .then_inc(xv_ready, 1)
                if c.exists():
                    pe.wait_ge(z_ready, c.count())
                    if m.exists():
                        pe.wait_ge(t_lo, m.count())
                    transpose(TP[0], z, zT)
                if m.exists():
                    pe.wait_ge(t_lo, m.count())
                    product(HID[m.slot], ops[:, 0, :, :, :], W1[:, T_, :, :, :], False, False)
                    pe.wait_ge(h_ready, m.count())
                    pe.wait_ge(s_lo, m.count())
                    transpose(TP[1], ht, hT)
                if c.exists():
                    pe.wait_ge(z_lo, c.count())
                    if c.plus(-2).exists():
                        pe.wait_ge(o_ready, c.count(extra=-1))
                    product(OUT[c.slot], zop, W2, True, True).then_inc(w2_done, 1)
                if m.exists():
                    product(HID[m.slot], ops[:, 1, :, :, :], W1[:, S_, :, :, :], False, False)
                    pe.wait_ge(h_lo, m.count())
                    product(HID[m.slot], ops[:, 2, :, :, :], W1[:, H, :, :, :], False, True).then_inc(hid_ready, 1)

            steps(pe, step)


def kernel(**inputs):
    import concourse.bacc as bacc
    from concourse.bass_utils import run_bass_kernel_spmd

    a = {n: np.asarray(v) for n, v in inputs.items()}

    def tiled(v):
        return v.reshape(B, S // P, P, *v.shape[2:])

    def put(rows, cols, *parts):
        r = np.zeros((rows, cols), np.float32)
        for i, j, v in parts:
            r[i:i + v.shape[0], j:j + v.shape[1]] = v
        return r

    x = tiled(a["x"])
    V, W_dec, b_dec = a["L0_cond_V"], a["L0_cond_W_dec"], a["L0_cond_b_dec"]
    L1 = {n[len("L1_cond_"):]: v for n, v in a.items() if n.startswith("L1_cond_")}
    path, comp, scale = (tiled(a[n]) for n in ("itok_BxS_0_999", "itok_BxS_0_4", "mask_BxS_ik0"))
    NDEC = D * RANK
    consts = put(P, P + 1, (0, 0, np.eye(P, dtype=np.float32)),
                 (0, P, (np.arange(P) % Q).astype(np.float32)[:, None]))
    batch_eye = np.eye(B, dtype=np.float32)
    spare = (RANK, 3 * Q + RANK)
    columns = [L1[f"{m}_{w}"].reshape(KC, P).T for w in ("b1", "b2", "g", "be") for m in ("mem", "noi", "res")]
    arrays = {
        "x": x,
        "xT": x.reshape(B, S // P, P, KC, P).transpose(0, 1, 4, 3, 2),
        "idx": np.stack([path, comp, scale], axis=-1),
        "rows": np.stack([comp, scale], axis=1),
        "consts": consts,
        "ubc": put(P, 3, *[(q * Q, 0, b_dec[NDEC:, None]) for q in (0, 2, 3)], *[(r, 1, batch_eye) for r in spare]),
        "selrow": put(1, P, *[(0, r, np.ones((1, B), np.float32)) for r in spare]),
        "int_b1": L1["int_b1"][None], "int_b2": L1["int_b2"][None], "int_g": L1["int_g"][None],
        "int_be": L1["int_be"][None], "aw": L1["aw"][None],
        "memT": a["cond_512"].T, "noiT": a["cond_64"].T, "resT": a["fside_Bx32_0"].T,
        "sv": np.concatenate(columns, axis=1),
        "bdec": b_dec[:NDEC].reshape(D, RANK),
        "wlast": put(MU, P, *[(0, q * Q, W_dec[:, NDEC:]) for q in (0, 2, 3)]),
        "W_dec": W_dec,
        "VT4": put(D, P, *[(0, q * Q, V.T) for q in range(4)]).reshape(KC, P, P).transpose(1, 0, 2),
        "V4": put(P, D, *[(q * Q, 0, V) for q in range(4)]),
        "BL": put(D, 3 * P, *[(0, q * Q, L1["cp_b"].T) for q in (0, 1)],
                  *[(0, P + q * Q, L1["tm_b"].T) for q in (0, 1)],
                  *[(0, 2 * P + q * Q, L1["ms_b"].T) for q in (2, 3)])
        .reshape(KC, P, 3, P).transpose(1, 2, 0, 3),
        "pw": np.concatenate([L1["pw_g"], L1["pw_b"]], axis=1),
        "ct": np.concatenate([L1["cp_g"], L1["tm_g"]], axis=1),
        "ms_g": L1["ms_g"],
        "int_W1": L1["int_W1"], "int_W2": L1["int_W2"],
    }
    for m in ("mem", "noi", "res"):
        arrays[f"{m}_W1"], arrays[f"{m}_W2"] = L1[f"{m}_W1"], L1[f"{m}_W2"]
    arrays = {n: np.ascontiguousarray(v) for n, v in arrays.items()}

    nc = bacc.Bacc("TRN2", target_bir_lowering=False, num_devices=1)
    d = {n: nc.dram_tensor("in_" + n, v.shape, mybir.dt.from_np(v.dtype), kind="ExternalInput").ap()
         for n, v in arrays.items()}
    out = nc.dram_tensor("out", (B, S, D), F32, kind="ExternalOutput").ap()
    build(nc, d, out)
    return run_bass_kernel_spmd(nc, [{"in_" + n: v for n, v in arrays.items()}], core_ids=[0]).results[0]["out"]
```

```python
from contextlib import ExitStack

import numpy as np
import concourse.bass as bass
from concourse import mybir

F32 = mybir.dt.float32
F32R = mybir.dt.float32r
I32 = mybir.dt.int32
ALU = mybir.AluOpType
ACT = mybir.ActivationFunctionType
AX = mybir.AxisListType

B, S, D = 2, 2048, 512
MU, NOI, RES = 256, 64, 32
RANK = 30
P = 128
KC = D // P
Q = 32
TILES = B * S // P
EPS = 1e-5
DECW = P * RANK
C = 3 * B
X, T_, S_, H = range(4)
HI, LO = 0, 1
WH, WT, WM, WN, WR, WS = range(6)
FIRST, LAST = 3, TILES - 3


class Tile:

    def __init__(self, s, i=None):
        self.s, self.i, self.slot, self.batch = s, i, s % 2, s % 2

    def plus(self, k):
        return Tile(self.s + k, self.i)

    def count(self, each=1, extra=1):
        v = (self.s + extra) * each
        return v if self.i is None else self.i * (2 * each) + v

    def slot_count(self, each):
        v = (self.s // 2 + 1) * each
        return v if self.i is None else self.i * each + v

    def pair(self):
        return self.s // 2 if self.i is None else self.i + self.s // 2

    def exists(self):
        return self.i is not None or 0 <= self.s < TILES


def steps(eng, emit):
    for n in range(-2, FIRST):
        emit(Tile(n))
    with eng.Fori(0, (LAST - FIRST) // 2) as i:
        emit(Tile(FIRST, i))
        emit(Tile(FIRST + 1, i))
    for n in range(LAST, TILES + 1):
        emit(Tile(n))


def build(nc, d, out):
    with ExitStack() as ctx:
        def sb(name, shape, dt=F32, c=ctx):
            return c.enter_context(nc.sbuf_tensor(name, shape, dt))

        W1 = sb("W1", [P, 4, 2, KC, D], F32R)
        W2 = sb("W2", [P, 2, KC, D], F32R)
        Ust = sb("Ust", [P, B, KC, P], F32R)
        Vst = sb("Vst", [P, D], F32R)
        VWst = sb("VWst", [P, D], F32R)
        BT = sb("BT", [P, D], F32R)
        ub = sb("ub", [P, B])
        ident = sb("ident", [P, P + 1])
        kept = dict(W1=W1, W2=W2, Ust=Ust, Vst=Vst, VWst=VWst, BT=BT, ub=ub, ident=ident)
        prepare(nc, d, kept)
        tiles(nc, d, out, kept)


def prepare(nc, d, k):
    W1, W2, Ust, Vst, VWst, BT, ub = k["W1"], k["W2"], k["Ust"], k["Vst"], k["VWst"], k["BT"], k["ub"]
    ident = k["ident"][:, 0:P]
    with ExitStack() as ctx:
        def sb(name, shape, dt=F32):
            return ctx.enter_context(nc.sbuf_tensor(name, shape, dt))

        def pb(name, shape):
            return ctx.enter_context(nc.psum_tensor(name, shape, F32))

        def sem(name):
            return ctx.enter_context(nc.semaphore(name))

        NSTAGE = 4
        HALF = DECW // 2
        BANK = HALF // 4
        PAIRS = 2 * KC
        raw = sb("raw", [P, 6, KC, D])
        stage = sb("stage", [P, NSTAGE, KC * D])
        Ur = sb("Ur", [P, DECW])
        Uf = sb("Uf", [P, KC, B, RANK])
        LM = sb("LM", [P, 3, KC, P])
        BL = sb("BL", [P, 3, KC, P])
        V4 = sb("V4", [P, D])
        cond = sb("cond", [P, 4, C])
        svr = raw[0:C, WS, :, :]
        hid, vec = (raw[0:C, WH, c, :] for c in range(2))
        bdec = sb("bdec", [P, KC, RANK])
        wlast = sb("wlast", [P, 2, P])
        ubc = sb("ubc", [P, 3])
        aw = sb("aw", [P, 6])
        wexp = sb("wexp", [P, 6])
        wsm = sb("wsm", [P, 6])
        sc = sb("sc", [P, 3])
        selr = sb("selr", [1, P + D])
        hidT = sb("hidT", [P, 3, KC, C])
        vst = sb("vst", [C, 6])
        vmv = sb("vmv", [C, 2])
        vrs = sb("vrs", [C, 3])

        pU = [pb(f"pU{g}", [P, 512]) for g in range(4)]
        pM = pb("pM", [P, D])
        pT = pb("pT", [P, 512])
        pVW = pb("pVW", [P, D])
        pBT = pb("pBT", [P, D])
        HIDT, VECT, ULAST = pT[:, 0:KC * C], pT[:, 64:64 + KC * C], pBT[:, 0:B]

        cond_in, mlp_in, sel_in, aw_in, late_in = (sem("cond_in"), sem("mlp_rows_in"), sem("sel_in"), sem("aw_in"),
                                                   sem("late_in"))
        raw_in = [sem(f"raw_in{i}") for i in range(6)]
        stage_in = [sem(f"stage_in{i}") for i in range(NSTAGE)]
        mlp_used = sem("mlp_used")
        half_used = sem("half_used")
        u_bank = sem("u_bank")
        u_row = sem("u_row")
        u_in = [sem(f"u_in{c}") for c in range(KC)]
        dve, pool_prep = sem("dve_prep"), sem("pool_prep")
        max_ready, exp_ready, w_ready = sem("max_ready"), sem("exp_ready"), sem("w_ready")
        pre_ready, hid_ready, hidT_sum, hidT_ready = (sem("pre_ready"), sem("hid_ready"), sem("hidT_sum"),
                                                      sem("hidT_ready"))
        mlp_sum, var_ready, rst_ready = sem("mlp_sum"), sem("var_ready"), sem("rst_ready")
        vec_ready, vecT_sum, lm_ready, bl_ready = sem("vec_ready"), sem("vecT_sum"), sem("lm_ready"), sem("bl_ready")
        zeroed, ulast_ready = sem("zeroed"), sem("ulast_ready")
        w1_hi, wx_ready, wx_hi, w2_hi = sem("w1_hi"), sem("wx_ready"), sem("wx_hi"), sem("w2_hi")
        bt_ready, vw_ready = sem("bt_ready"), sem("vw_ready")

        def load(eng, got, *pairs):
            for dst, src in pairs:
                eng.dma_start(dst, src).then_inc(got, 16)

        DEC = [("dec", j) for j in range(2 * PAIRS)]
        MLP2 = [("mlp2", m) for m in range(3)]
        ring = [("mlp1", 0)] + DEC[:4] + MLP2 + DEC[4:] + [("int2", 0)]
        slot = {item: i % NSTAGE for i, item in enumerate(ring)}
        arrived = {item: 16 * (i // NSTAGE + 1) for i, item in enumerate(ring)}
        then_raw = {("dec", 5 + n): blk for n, blk in enumerate((WM, WN, WR, WT, WS, WH))}

        def source(item):
            kind, j = item
            if kind == "mlp1":
                return d["mlp_W1"]
            if kind == "mlp2":
                return d[("mem_W2", "noi_W2", "res_W2")[j]].rearrange("(c p) n -> p c n", p=P)
            if kind == "int2":
                return d["int_W2"].rearrange("(c p) n -> p c n", p=P)
            return d["W_dec"][j % 2 * P:(j % 2 + 1) * P, j // 2 * HALF:(j // 2 + 1) * HALF]

        def read(item):
            kind, j = item
            if kind == "mlp1":
                return mlp_used, 1
            if kind == "mlp2":
                return mlp_used, 2 + j
            return (u_bank, 4 * (j // 2 + 1)) if j % 2 else (half_used, j // 2 + 1)

        def staged(item):
            s = stage[:, slot[item], :]
            return s[:, 0:HALF] if item[0] == "dec" else s.rearrange("p (c n) -> p c n", n=D)

        block = ctx.enter_context(nc.Block())

        @block.sync
        def _(sp):
            for i, item in enumerate(ring):
                if i >= NSTAGE:
                    sp.wait_ge(*read(ring[i - NSTAGE]))
                load(sp, stage_in[slot[item]], (staged(item), source(item)))
                if item in then_raw:
                    blk = then_raw[item]
                    if blk == WS:
                        sp.wait_ge(vecT_sum, 1)
                    load(sp, raw_in[blk], (raw[:, blk, :, :],
                                           d["int_W1"][blk * D:(blk + 1) * D, :].rearrange("(c p) n -> p c n", p=P)))

        @block.scalar
        def _(act):
            load(act, cond_in, (cond[:, :, :], d["cond"]), (k["ident"][:, :], d["consts"][:, 0:P + 1]))
            load(act, mlp_in, (svr[:, :, :], d["svr"]))
            load(act, aw_in, (aw[:, :], d["aw"].to_broadcast([P, 6])))
            load(act, sel_in, (wlast[:, :, :], d["wlast"].rearrange("(c p) r -> p c r", p=P)), (ubc[:, :], d["ubc"]),
                 (selr[0:1, 0:P], d["selrow"]), (selr[0:1, P:P + D], d["int_b1"]),
                 (bdec[:, :, :], d["bdec"].rearrange("(c p) r -> p c r", p=P)))
            load(act, late_in, (V4[:, :], d["V4"]), (BL[:, :, :, :], d["BL"]),
                 *[(LM[:, m, :, :], d["VT4"]) for m in range(3)])
            act.wait_ge(max_ready, 1)
            nc.scalar.activation(wexp[:, :], aw[:, :], ACT.Exp, bias=sc[:, 0:1],
                                 accum_out=sc[:, 1:2]).then_inc(exp_ready, 1)
            act.wait_ge(pre_ready, 1)
            nc.scalar.activation(hid[:, :], hid[:, :], ACT.Silu, bias=0.0).then_inc(hid_ready, 1)

            def high_part(blk, src):
                act.wait_ge(raw_in[src], 16)
                nc.scalar.activation(W1[:, blk, HI, :, :], raw[:, src, :, :], ACT.Copy,
                                     scale=wsm[:, src:src + 1]).then_inc(w1_hi, 1)

            for pair in range(PAIRS):
                c, h = divmod(pair, 2)
                for g in range(4):
                    act.wait_ge(u_bank, 4 * pair + g + 1)
                    col = h * HALF + g * BANK
                    nc.scalar.activation(Ur[c * Q:c * Q + B, col:col + BANK], pU[g][0:B, 0:BANK],
                                         ACT.Copy).then_inc(u_row, 1)
                if h == 1:
                    act.wait_ge(u_row, 4 * (pair + 1))
                    for b in range(B):
                        row = Ur[c * Q + b:c * Q + b + 1, :].rearrange("o (p r) -> o p r", r=RANK)
                        load(act, u_in[c], (Uf[:, c, b, :], row))
                if pair == 4:
                    act.wait_ge(w_ready, 1)
                    high_part(T_, WT)
                if pair == 5:
                    high_part(S_, WS)
                if pair == 6:
                    high_part(H, WH)
                    act.wait_ge(wx_ready, 3)
                    nc.scalar.activation(W1[:, X, HI, :, :], raw[:, WM, :, :], ACT.Copy).then_inc(wx_hi, 1)
            act.wait_ge(stage_in[slot[("int2", 0)]], arrived[("int2", 0)])
            nc.scalar.activation(W2[:, HI, :, :], staged(("int2", 0)), ACT.Copy).then_inc(w2_hi, 1)

        @block.tensor
        def _(pe):
            def wait_for(item):
                pe.wait_ge(stage_in[slot[item]], arrived[item])

            def decode(*items):
                for item in items:
                    pair, m = divmod(item[1], 2)
                    wait_for(item)
                    for g in range(4):
                        if m == 0 and pair > 0:
                            pe.wait_ge(u_row, 4 * (pair - 1) + g + 1)
                        last = nc.tensor.matmul(pU[g][0:B, 0:BANK], cond[:, m, 0:B],
                                                staged(item)[:, g * BANK:(g + 1) * BANK], start=(m == 0), stop=(m == 1))
                        if m == 1:
                            last.then_inc(u_bank, 1)
                    if m == 0:
                        last.then_inc(half_used, 1)

            pe.wait_ge(cond_in, 32)
            wait_for(("mlp1", 0))
            for c in range(4):
                last = nc.tensor.matmul(pM[0:C, :], cond[:, c, :], staged(("mlp1", 0))[:, c, :],
                                        start=(c == 0), stop=(c == 3))
            last.then_inc(mlp_used, 1)
            decode(*DEC[0:2])
            pe.wait_ge(hid_ready, 1)
            for c in range(KC):
                last = nc.tensor.transpose(HIDT[:, c * C:(c + 1) * C], hid[:, c * P:(c + 1) * P], ident[0:C, 0:C])
            last.then_inc(hidT_sum, 1)
            pe.wait_ge(sel_in, 16 * 5)
            for m in range(2):
                last = nc.tensor.matmul(ULAST, wlast[:, m, :], cond[:, m, 0:B], start=(m == 0), stop=(m == 1))
            last.then_inc(ulast_ready, 1)
            decode(*DEC[2:4])
            pe.wait_ge(hidT_ready, 3)
            for m in range(3):
                wait_for(MLP2[m])
                for c in range(KC):
                    last = nc.tensor.matmul(pM[0:C, :], hidT[:, m, c, :], staged(MLP2[m])[:, c, :],
                                            start=(m == 0 and c == 0), stop=(m == 2 and c == KC - 1))
                last.then_inc(mlp_used, 1)
            decode(*DEC[4:8])
            pe.wait_ge(vec_ready, 1)
            for c in range(KC):
                last = nc.tensor.transpose(VECT[:, c * C:(c + 1) * C], vec[:, c * P:(c + 1) * P], ident[0:C, 0:C])
            last.then_inc(vecT_sum, 1)
            decode(*DEC[8:11])
            pe.wait_ge(lm_ready, 2)
            nc.tensor.matmul(pVW[:, :], selr[0:1, 0:P], selr[0:1, P:P + D], start=True, stop=False)
            for m, blk in enumerate((WM, WN, WR)):
                pe.wait_ge(raw_in[blk], 16)
                for c in range(KC):
                    last = nc.tensor.matmul(pVW[:, :], LM[:, m, c, :], raw[:, blk, c, :],
                                            start=False, stop=(m == 2 and c == KC - 1))
            last.then_inc(vw_ready, 1)
            decode(*DEC[11:])
            pe.wait_ge(bl_ready, 3)
            for t, blk in enumerate((WH, WT, WS)):
                pe.wait_ge(raw_in[blk], 16)
                for c in range(KC):
                    last = nc.tensor.matmul(pBT[:, :], BL[:, t, c, :], raw[:, blk, c, :],
                                            start=(t == 0 and c == 0), stop=(t == 2 and c == KC - 1))
            last.then_inc(bt_ready, 1)

        @block.gpsimd
        def _(pool):
            nc.gpsimd.memset(hidT[:, :, :, :], 0.0).then_inc(zeroed, 1)
            nc.gpsimd.memset(vrs[:, 1:2], -0.5).then_inc(pool_prep, 1)
            nc.gpsimd.memset(Ust[:, :, :, :].bitcast(F32), 0.0).then_inc(zeroed, 1)
            pool.wait_ge(pool_prep, 1)
            pool.wait_ge(var_ready, 1)
            nc.gpsimd.tensor_tensor(vrs[:, 2:3], vrs[:, 0:1], vrs[:, 1:2], ALU.pow).then_inc(rst_ready, 1)
            pool.wait_ge(wx_hi, 1)
            nc.gpsimd.tensor_tensor(W1[:, X, LO, :, :], raw[:, WM, :, :], W1[:, X, HI, :, :].bitcast(F32),
                                    ALU.subtract)
            pool.wait_ge(w2_hi, 1)
            nc.gpsimd.tensor_tensor(W2[:, LO, :, :], staged(("int2", 0)), W2[:, HI, :, :].bitcast(F32), ALU.subtract)

        @block.vector
        def _(v):
            seen = [0]

            def link(ins):
                seen[0] += 1
                ins.then_inc(dve, 1)
                v.wait_ge(dve, seen[0])

            v.wait_ge(mlp_in, 16)
            v.wait_ge(mlp_used, 1)
            nc.vector.tensor_tensor(hid[:, :], pM[0:C, :], svr[:, 0, :], ALU.add).then_inc(pre_ready, 1)
            v.wait_ge(aw_in, 16)
            nc.vector.tensor_reduce(sc[:, 0:1], aw[:, :], axis=AX.X, op=ALU.max, negate=True).then_inc(max_ready, 1)
            v.wait_ge(exp_ready, 1)
            link(nc.vector.reciprocal(sc[:, 2:3], sc[:, 1:2]))
            nc.vector.tensor_scalar(wsm[:, :], wexp[:, :], sc[:, 2:3], None, ALU.mult).then_inc(w_ready, 1)
            v.wait_ge(zeroed, 2)
            v.wait_ge(hidT_sum, 1)
            for m in range(3):
                nc.vector.tensor_copy(hidT[:, m, :, m * B:(m + 1) * B],
                                      HIDT.rearrange("p (c j) -> p c j", j=C)[:, :, m * B:(m + 1) * B]) \
                    .then_inc(hidT_ready, 1)
            v.wait_ge(sel_in, 16 * 5)
            v.wait_ge(ulast_ready, 1)
            nc.vector.scalar_tensor_tensor(out=ub[:, :], in0=ULAST, scalar=ubc[:, 0:1], in1=ubc[:, 1:3],
                                           op0=ALU.add, op1=ALU.add)
            v.wait_ge(late_in, 16 * 5)
            link(nc.vector.tensor_copy(Vst[:, :], V4[:, :]))
            nc.vector.tensor_tensor(Vst[3 * Q:P, :], V4[3 * Q:P, :], Vst[3 * Q:P, :].bitcast(F32), ALU.subtract)
            v.wait_ge(w_ready, 1)
            for t, blk in enumerate((WH, WT, WS)):
                nc.vector.tensor_scalar(BL[:, t, :, :], BL[:, t, :, :], wsm[:, blk:blk + 1], None,
                                        ALU.mult).then_inc(bl_ready, 1)
            for m, blk in enumerate((WM, WN, WR)):
                last = nc.vector.tensor_scalar(LM[:, m, :, :], LM[:, m, :, :], wsm[:, blk:blk + 1], None, ALU.mult)
            last.then_inc(lm_ready, 1)
            v.wait_ge(mlp_used, 4)
            link(nc.vector.tensor_tensor(vec[:, :], pM[0:C, :], svr[:, 1, :], ALU.add))
            link(nc.vector.bn_stats(vst[:, :], vec[:, :]))
            link(nc.vector.bn_aggr(vmv[:, :], vst[:, :]))
            nc.vector.tensor_scalar(vrs[:, 0:1], vmv[:, 1:2], EPS, None, ALU.add).then_inc(var_ready, 1)
            v.wait_ge(rst_ready, 1)
            link(nc.vector.tensor_scalar(vec[:, :], vec[:, :], vmv[:, 0:1], vrs[:, 2:3], ALU.subtract, ALU.mult))
            link(nc.vector.tensor_tensor(vec[:, :], vec[:, :], svr[:, 2, :], ALU.mult))
            nc.vector.tensor_tensor(vec[:, :], vec[:, :], svr[:, 3, :], ALU.add).then_inc(vec_ready, 1)
            v.wait_ge(vecT_sum, 1)
            v.wait_ge(lm_ready, 1)
            for m, blk in enumerate((WM, WN, WR)):
                for col in (RANK, 3 * Q + RANK):
                    last = nc.vector.tensor_scalar(LM[:, m, :, col:col + B],
                                                   VECT.rearrange("p (c j) -> p c j", j=C)[:, :, m * B:(m + 1) * B],
                                                   wsm[:, blk:blk + 1], None, ALU.mult)
            last.then_inc(lm_ready, 1)

            def low_part(n, blk, src):
                v.wait_ge(w1_hi, n)
                nc.vector.scalar_tensor_tensor(out=W1[:, blk, LO, :, :], in0=raw[:, src, :, :],
                                               scalar=wsm[:, src:src + 1], in1=W1[:, blk, HI, :, :].bitcast(F32),
                                               op0=ALU.mult, op1=ALU.subtract)

            def features(c):
                v.wait_ge(u_in[c], 16 * B)
                for b in range(B):
                    last = nc.vector.tensor_tensor(Uf[:, c, b, :], Uf[:, c, b, :], bdec[:, c, :], ALU.add)
                link(last)
                for q in (2, 3, 0):
                    last = nc.vector.tensor_copy(Ust[:, :, c, q * Q:q * Q + RANK], Uf[:, c, :, :])
                link(last)
                nc.vector.tensor_tensor(Ust[:, :, c, Q:Q + RANK], Uf[:, c, :, :],
                                        Ust[:, :, c, 0:RANK].bitcast(F32), ALU.subtract)

            features(0)
            features(1)
            low_part(1, T_, WT)
            low_part(2, S_, WS)
            features(2)
            wx = raw[:, WM, :, :]
            v.wait_ge(vw_ready, 1)
            v.wait_ge(raw_in[WM], 16)
            nc.vector.tensor_scalar(wx, raw[:, WM, :, :], wsm[:, WM:WM + 1], None, ALU.mult).then_inc(wx_ready, 1)
            for n, blk in enumerate((WN, WR)):
                v.wait_ge(raw_in[blk], 16)
                v.wait_ge(wx_ready, n + 1)
                nc.vector.scalar_tensor_tensor(out=wx, in0=raw[:, blk, :, :], scalar=wsm[:, blk:blk + 1], in1=wx,
                                               op0=ALU.mult, op1=ALU.add).then_inc(wx_ready, 1)
            link(nc.vector.tensor_copy(VWst[:, :], pVW[:, :]))
            nc.vector.tensor_tensor(VWst[3 * Q:P, :], pVW[3 * Q:P, :], VWst[3 * Q:P, :].bitcast(F32), ALU.subtract)
            low_part(3, H, WH)
            features(3)
            v.wait_ge(bt_ready, 1)
            link(nc.vector.tensor_copy(BT[:, :], pBT[:, :]))
            for q in (1, 3):
                nc.vector.tensor_tensor(BT[q * Q:(q + 1) * Q, :], pBT[q * Q:(q + 1) * Q, :],
                                        BT[q * Q:(q + 1) * Q, :].bitcast(F32), ALU.subtract)


def tiles(nc, d, out, k):
    W1, W2, Ust, Vst, VWst, BT, ub = k["W1"], k["W2"], k["Ust"], k["Vst"], k["VWst"], k["BT"], k["ub"]
    ident, inquad = k["ident"][:, 0:P], k["ident"][:, P:P + 1]
    with ExitStack() as ctx:
        def sb(name, shape, dt=F32):
            return ctx.enter_context(nc.sbuf_tensor(name, shape, dt))

        def pb(name, shape):
            return ctx.enter_context(nc.psum_tensor(name, shape, F32))

        def sem(name):
            return ctx.enter_context(nc.semaphore(name))

        def sem2(name):
            return [sem(f"{name}{i}") for i in range(2)]

        b2bc, gbc, bebc = (sb(name, [P, D]) for name in ("b2bc", "gbc", "bebc"))
        xT = sb("xT", [P, 2, KC, P])
        xop = sb("xop", [P, 2, 2, KC, P], F32R)
        x0 = sb("x0", [P, 2, D])
        idx = sb("idx", [P, 2, 3], I32)
        idxrep = sb("idxrep", [P, 2, P], I32)
        OH = sb("OH", [P, 2, P], F32R)
        stack = sb("stack", [P, 2, P], F32R)
        inner = sb("inner", [P, P])
        x1 = sb("x1", [P, 2, D])
        xb = sb("xb", [P, 2, D])
        xhat = sb("xhat", [P, 2, D])
        pwt = sb("pwt", [P, 2, 2 * D])
        ctt = sb("ctt", [P, 2, 2 * D])
        sgt = sb("sgt", [P, 2, D])
        tt = sb("tt", [P, D])
        st = sb("st_", [P, D])
        h1 = sb("h1", [P, D])
        hn = sb("hn", [P, D])
        ht = sb("ht", [P, D])
        ops = sb("ops", [P, 3, 2, KC, P], F32R)
        z = sb("z", [P, D])
        zop = sb("zop", [P, 2, KC, P], F32R)
        o = sb("o", [P, D])
        u = sb("u", [P, D])
        y = sb("y", [P, 2, D])
        bn = sb("bn", [P, 3, 6])
        mv = sb("mv", [P, 3, 2])
        ve = sb("ve", [P, 3])
        rs = sb("rs", [P, 3])
        mhalf = sb("mhalf_", [P, 1])
        warm = sb("warm", [P, 1])

        HID = [pb(f"HID{i}", [P, D]) for i in range(2)]
        OUT = [pb(f"OUT{i}", [P, D]) for i in range(2)]
        TP = [pb(f"TP{i}", [P, D]) for i in range(2)]
        XU = pb("XU", [P, 512])
        XV = pb("XV", [P, D])

        xT_in, x0_in, idx_in, rep_in = sem2("xT_in"), sem2("x0_in"), sem2("idx_in"), sem2("rep_in")
        pw_in, ct_in, sg_in, stored = sem2("pw_in"), sem2("ct_in"), sem2("sg_in"), sem2("stored")
        x_hi, x_lo, x_used, oh_ready = sem("x_hi"), sem("x_lo"), sem("x_used"), sem("oh_ready")
        inner_part, inner_ready = sem("inner_part"), sem("inner_ready")
        xu_ready, stack_part, stack_ready, xv_ready = sem("xu_ready"), sem("stack_part"), sem("stack_ready"), sem("xv_ready")
        x1_ready, bn_done, mv1_ready, r1_ready = sem("x1_ready"), sem("bn_done"), sem("mv1_ready"), sem("r1_ready")
        xhat_ready, t_ready, s_ready, h1_part, h1_ready = (sem("xhat_ready"), sem("t_ready"), sem("s_ready"),
                                                           sem("h1_part"), sem("h1_ready"))
        mv2_ready, r2_ready, hn_ready, h_ready = sem("mv2_ready"), sem("r2_ready"), sem("hn_ready"), sem("h_ready")
        tT, sT, hT, zT = sem("tT"), sem("sT"), sem("hT"), sem("zT")
        t_hi, s_hi, h_hi, z_hi = sem("t_hi"), sem("s_hi"), sem("h_hi"), sem("z_hi")
        t_lo, s_lo, h_lo, z_lo = sem("t_lo"), sem("s_lo"), sem("h_lo"), sem("z_lo")
        hid_ready, z_ready, w2_done, o_ready = sem("hid_done"), sem("z_ready"), sem("w2_done"), sem("o_ready")
        mv3_ready, r3_ready, xb_ready, u_ready, y_ready = (sem("mv3_ready"), sem("r3_ready"), sem("xb_ready"),
                                                           sem("u_done"), sem("y_ready"))
        pool_part, mhalf_ready = sem("pool_part"), sem("mhalf_ready")
        rows_in = sem("rows_in")
        block = ctx.enter_context(nc.Block())

        outv = out.rearrange("b (j p) n -> b j p n", p=P)

        @block.sync
        def _(sp):
            def step(n):
                a = n.plus(2)
                if a.exists():
                    s, old = a.slot, a.plus(-2)
                    if old.exists():
                        sp.wait_ge(x_lo, old.count())
                    sp.dma_start(xT[:, s, :, :], d["xT"][s, bass.ds(a.pair(), 1), :, :, :].rearrange(
                        "o p c t -> (o p) c t")).then_inc(xT_in[s], 16)
                    if old.exists():
                        sp.wait_ge(x1_ready, old.count())
                    sp.dma_start(x0[:, s, :], d["x"][s, bass.ds(a.pair(), 1), :, :].rearrange("o p n -> (o p) n")) \
                      .then_inc(x0_in[s], 16)
                    if old.exists():
                        sp.wait_ge(sg_in[s], old.slot_count(16))
                        sp.wait_ge(ct_in[s], old.slot_count(16))
                        sp.wait_ge(pw_in[s], old.slot_count(16))
                    sp.dma_start(idx[:, s, :], d["idx"][s, bass.ds(a.pair(), 1), :, :].rearrange("o p n -> (o p) n")) \
                      .then_inc(idx_in[s], 16)
                    if old.exists():
                        sp.wait_ge(oh_ready, old.count())
                    for half in range(2):
                        sp.dma_start(idxrep[half * P // 2:(half + 1) * P // 2, s, :],
                                     d["rows"][s, half, bass.ds(a.pair(), 1), :].to_broadcast([P // 2, P])) \
                          .then_inc(rep_in[s], 16)
                if n.plus(-2).exists():
                    store(n.plus(-2))

            def store(c):
                sp.wait_ge(y_ready, c.count())
                sp.dma_start(outv[c.batch, bass.ds(c.pair(), 1), :, :].rearrange("o p n -> (o p) n"),
                             y[:, c.slot, :]).then_inc(stored[c.slot], 16)

            steps(sp, step)
            store(Tile(TILES - 1))
            for s in range(2):
                sp.wait_ge(stored[s], 16 * TILES // 2)

        @block.gpsimd
        def _(pool):
            nc.gpsimd.memset(mhalf[:, :], -0.5).then_inc(mhalf_ready, 1)

            def rstd(which, t, have, done):
                pool.wait_ge(have, t.count())
                pool.nop(nofuse=True)
                nc.gpsimd.tensor_scalar(ve[:, which:which + 1], mv[:, which, 1:2], EPS, 1.0, ALU.add, ALU.mult) \
                    .then_inc(pool_part, 1)
                parts[0] += 1
                pool.wait_ge(pool_part, part_count(t))
                nc.gpsimd.tensor_tensor(rs[:, which:which + 1], ve[:, which:which + 1], mhalf[:, :],
                                        ALU.pow).then_inc(done, 1)

            parts = [0]
            base = [0, None]

            def part_count(t):
                return parts[0] if base[1] is None else base[1] * base[0] + parts[0]

            def step(n):
                a, f, c = n.plus(2), n.plus(1), n.plus(-1)
                if a.exists():
                    s, old = a.slot, a.plus(-2)
                    pool.wait_ge(idx_in[s], a.slot_count(16))
                    if old.exists():
                        pool.wait_ge(h_ready, old.count())
                    pool.nop(nofuse=True)
                    for dst, table, col, got in ((ctt[:, s, :], d["ct"], 1, ct_in), (sgt[:, s, :], d["ms_g"], 2, sg_in),
                                                 (pwt[:, s, :], d["pw"], 0, pw_in)):
                        pool.indirect_dma_start(out=dst, out_offset=None, in_=table,
                                                in_offset=bass.IndirectOffsetOnAxis(ap=idx[:, s, col:col + 1], axis=0)) \
                            .then_inc(got[s], 16)
                if f.exists():
                    s = f.slot
                    rstd(0, f, mv1_ready, r1_ready)
                    pool.wait_ge(xhat_ready, f.count())
                    pool.wait_ge(pw_in[s], f.slot_count(16))
                    if f.plus(-1).exists():
                        pool.wait_ge(hn_ready, f.count(extra=0))
                    nc.gpsimd.tensor_tensor(h1[:, :], xhat[:, s, :], pwt[:, s, 0:D], ALU.mult).then_inc(h1_part, 1)
                    pool.wait_ge(h1_part, f.count())
                    nc.gpsimd.tensor_tensor(h1[:, :], h1[:, :], pwt[:, s, D:2 * D], ALU.add).then_inc(h1_ready, 1)
                if a.exists():
                    s = a.slot
                    pool.wait_ge(x_hi, a.count())
                    nc.gpsimd.tensor_tensor(xop[:, s, LO, :, :], xT[:, s, :, :], xop[:, s, HI, :, :].bitcast(F32),
                                            ALU.subtract).then_inc(x_lo, 1)
                if f.exists():
                    rstd(1, f, mv2_ready, r2_ready)
                if c.exists():
                    rstd(2, c, mv3_ready, r3_ready)
                if f.exists():
                    s = f.slot
                    if f.plus(-2).exists():
                        pool.wait_ge(y_ready, f.count(extra=-1))
                    pool.wait_ge(x1_ready, f.count())
                    nc.gpsimd.tensor_tensor(xb[:, s, :], x1[:, s, :], bebc[:, :], ALU.add).then_inc(xb_ready, 1)

            pool.wait_ge(mhalf_ready, 1)
            pool.wait_ge(rows_in, 48)
            for n in range(-2, FIRST):
                step(Tile(n))
            with pool.Fori(0, (LAST - FIRST) // 2) as i:
                before = parts[0]
                base[:] = [6, i]
                step(Tile(FIRST, i))
                step(Tile(FIRST + 1, i))
                assert parts[0] - before == 6
            parts[0] = before + 6 * ((LAST - FIRST) // 2)
            base[1] = None
            for n in range(LAST, TILES + 1):
                step(Tile(n))

        @block.scalar
        def _(act):
            for row, name in ((bebc, "int_be"), (b2bc, "int_b2"), (gbc, "int_g")):
                act.dma_start(row[:, :], d[name].to_broadcast([P, D])).then_inc(rows_in, 16)
            nc.scalar.activation(warm[:, :], ident[:, 0:1], ACT.Silu, bias=0.0)

            def split_hi(dst, bank, have, t, done):
                act.wait_ge(have, t.count())
                nc.scalar.activation(dst.rearrange("p c t -> p (c t)"), bank[:, :], ACT.Copy).then_inc(done, 1)

            def step(n):
                a, m, c = n.plus(2), n, n.plus(-1)
                if m.exists():
                    split_hi(ops[:, 0, HI, :, :], TP[0], tT, m, t_hi)
                    split_hi(ops[:, 1, HI, :, :], TP[1], sT, m, s_hi)
                if a.exists():
                    s, old = a.slot, a.plus(-2)
                    act.wait_ge(xT_in[s], a.slot_count(16))
                    if old.exists():
                        act.wait_ge(x_used, old.count())
                    nc.scalar.activation(xop[:, s, HI, :, :], xT[:, s, :, :], ACT.Copy).then_inc(x_hi, 1)
                if c.exists():
                    split_hi(zop[:, HI, :, :], TP[0], zT, c, z_hi)
                if m.exists():
                    split_hi(ops[:, 2, HI, :, :], TP[1], hT, m, h_hi)
                    act.wait_ge(hid_ready, m.count())
                    nc.scalar.activation(z[:, :], HID[m.slot][:, :], ACT.Silu, bias=0.0).then_inc(z_ready, 1)

            steps(act, step)

        @block.vector
        def _(v):
            def split_lo(dst, hi, bank, have, t, done):
                v.wait_ge(have, t.count())
                nc.vector.tensor_tensor(dst.rearrange("p c t -> p (c t)"), bank[:, :],
                                        hi.bitcast(F32).rearrange("p c t -> p (c t)"), ALU.subtract).then_inc(done, 1)

            def stats(which, src, t, before, ready):
                nc.vector.bn_stats(bn[:, which, :], src).then_inc(bn_done, 1)
                parts[0] += 1
                v.wait_ge(bn_done, parts[0] if base[1] is None else base[1] * base[0] + parts[0])
                v.nop(nofuse=True)
                nc.vector.bn_aggr(mv[:, which, :], bn[:, which, :]).then_inc(ready, 1)

            parts = [0]
            base = [0, None]

            def step(n):
                a, f, m, c = n.plus(2), n.plus(1), n, n.plus(-1)
                if f.exists():
                    s, bias = f.slot, ub[:, f.batch:f.batch + 1]
                    v.wait_ge(xu_ready, f.count())
                    nc.vector.tensor_scalar(inner[:, :], XU[:, 0:P], bias, None, ALU.add).then_inc(inner_part, 1)
                    v.wait_ge(inner_part, f.count())
                    nc.vector.tensor_tensor(inner[:, :], inner[:, :], XU[:, P:2 * P], ALU.add).then_inc(inner_ready, 1)
                    v.wait_ge(inner_ready, f.count())
                    if f.plus(-2).exists():
                        v.wait_ge(x_used, f.count(extra=-1))
                    nc.vector.tensor_copy(stack[:, s, :], inner[:, :]).then_inc(stack_part, 1)
                    v.wait_ge(stack_part, f.count())
                    nc.vector.tensor_tensor(stack[2 * Q:3 * Q, s, :], inner[2 * Q:3 * Q, :],
                                            stack[2 * Q:3 * Q, s, :].bitcast(F32), ALU.subtract) \
                        .then_inc(stack_ready, 1)
                if m.exists():
                    split_lo(ops[:, 0, LO, :, :], ops[:, 0, HI, :, :], TP[0], t_hi, m, t_lo)
                    split_lo(ops[:, 1, LO, :, :], ops[:, 1, HI, :, :], TP[1], s_hi, m, s_lo)
                if a.exists():
                    s = a.slot
                    v.wait_ge(rep_in[s], a.slot_count(32))
                    if m.exists():
                        v.wait_ge(x_used, m.count())
                    nc.vector.tensor_scalar(OH[:, s, :], idxrep[:, s, :], inquad, None, ALU.is_equal).then_inc(oh_ready, 1)
                if f.exists():
                    s = f.slot
                    v.wait_ge(xv_ready, f.count())
                    v.wait_ge(x0_in[s], f.slot_count(16))
                    if f.plus(-2).exists():
                        v.wait_ge(xb_ready, f.count(extra=-1))
                    nc.vector.tensor_tensor(x1[:, s, :], XV[:, :], x0[:, s, :], ALU.add).then_inc(x1_ready, 1)
                if c.exists():
                    split_lo(zop[:, LO, :, :], zop[:, HI, :, :], TP[0], z_hi, c, z_lo)
                if f.exists():
                    v.wait_ge(x1_ready, f.count())
                    stats(0, x1[:, f.slot, :], f, 0, mv1_ready)
                if f.exists():
                    s = f.slot
                    v.wait_ge(r1_ready, f.count())
                    if f.plus(-2).exists():
                        v.wait_ge(h1_part, f.count(extra=-1))
                    nc.vector.tensor_scalar(xhat[:, s, :], x1[:, s, :], mv[:, 0, 0:1], rs[:, 0:1],
                                            ALU.subtract, ALU.mult).then_inc(xhat_ready, 1)
                    v.wait_ge(xhat_ready, f.count())
                    v.wait_ge(ct_in[s], f.slot_count(16))
                    if m.exists():
                        v.wait_ge(tT, m.count())
                    nc.vector.tensor_tensor(tt[:, :], xhat[:, s, :], ctt[:, s, D:2 * D], ALU.mult).then_inc(t_ready, 1)
                    v.wait_ge(sg_in[s], f.slot_count(16))
                    if m.exists():
                        v.wait_ge(sT, m.count())
                    nc.vector.tensor_tensor(st[:, :], xhat[:, s, :], sgt[:, s, :], ALU.mult).then_inc(s_ready, 1)
                if m.exists():
                    split_lo(ops[:, 2, LO, :, :], ops[:, 2, HI, :, :], TP[1], h_hi, m, h_lo)
                if f.exists():
                    v.wait_ge(h1_ready, f.count())
                    stats(1, h1[:, :], f, 0, mv2_ready)
                if c.exists():
                    v.wait_ge(w2_done, c.count())
                    nc.vector.tensor_tensor(o[:, :], OUT[c.slot][:, :], b2bc[:, :], ALU.add).then_inc(o_ready, 1)
                    v.wait_ge(o_ready, c.count())
                    stats(2, o[:, :], c, 0, mv3_ready)
                if f.exists():
                    v.wait_ge(r2_ready, f.count())
                    nc.vector.tensor_scalar(hn[:, :], h1[:, :], mv[:, 1, 0:1], rs[:, 1:2],
                                            ALU.subtract, ALU.mult).then_inc(hn_ready, 1)
                if c.exists():
                    v.wait_ge(mv3_ready, c.count())
                    nc.vector.scalar_tensor_tensor(out=u[:, :], in0=o[:, :], scalar=mv[:, 2, 0:1], in1=gbc[:, :],
                                                   op0=ALU.subtract, op1=ALU.mult).then_inc(u_ready, 1)
                if f.exists():
                    v.wait_ge(hn_ready, f.count())
                    nc.vector.tensor_tensor(ht[:, :], hn[:, :], ctt[:, f.slot, 0:D], ALU.mult).then_inc(h_ready, 1)
                if c.exists():
                    s = c.slot
                    v.wait_ge(u_ready, c.count())
                    v.wait_ge(r3_ready, c.count())
                    v.wait_ge(xb_ready, c.count())
                    if c.plus(-2).exists():
                        v.wait_ge(stored[s], c.plus(-2).slot_count(16))
                    nc.vector.scalar_tensor_tensor(out=y[:, s, :], in0=u[:, :], scalar=rs[:, 2:3], in1=xb[:, s, :],
                                                   op0=ALU.mult, op1=ALU.add).then_inc(y_ready, 1)

            v.wait_ge(rows_in, 48)
            for n in range(-2, FIRST):
                step(Tile(n))
            with v.Fori(0, (LAST - FIRST) // 2) as i:
                before = parts[0]
                base[:] = [6, i]
                step(Tile(FIRST, i))
                step(Tile(FIRST + 1, i))
                assert parts[0] - before == 6
            parts[0] = before + 6 * ((LAST - FIRST) // 2)
            base[1] = None
            for n in range(LAST, TILES + 1):
                step(Tile(n))

        @block.tensor
        def _(pe):
            def transpose(dst, src, done):
                for c in range(KC):
                    last = nc.tensor.transpose(dst[:, c * P:(c + 1) * P], src[:, c * P:(c + 1) * P], ident)
                last.then_inc(done, 1)

            def product(bank, op, w, start, stop):
                for c in range(KC):
                    nc.tensor.matmul(bank[:, :], op[:, HI, c, :], w[:, HI, c, :], start=start and c == 0, stop=False)
                    nc.tensor.matmul(bank[:, :], op[:, HI, c, :], w[:, LO, c, :], start=False, stop=False)
                    last = nc.tensor.matmul(bank[:, :], op[:, LO, c, :], w[:, HI, c, :], start=False,
                                            stop=stop and c == KC - 1)
                return last

            def step(n):
                f, m, c = n.plus(1), n, n.plus(-1)
                if m.exists():
                    pe.wait_ge(t_ready, m.count())
                    if m.plus(-2).exists():
                        pe.wait_ge(z_lo, m.count(extra=-1))
                    transpose(TP[0], tt, tT)
                    pe.wait_ge(s_ready, m.count())
                    if m.plus(-1).exists():
                        pe.wait_ge(h_lo, m.count(extra=0))
                    transpose(TP[1], st, sT)
                if f.exists():
                    pe.wait_ge(x_lo, f.count())
                    if m.exists():
                        pe.wait_ge(stack_ready, m.count())
                    for q in range(KC):
                        last = nc.tensor.matmul(XU[:, 0:2 * P], Ust[:, f.batch, q, :], xop[:, f.slot, :, q, :],
                                                start=(q == 0), stop=(q == KC - 1))
                    last.then_inc(xu_ready, 1)
                if m.exists():
                    if m.plus(-2).exists():
                        pe.wait_ge(z_ready, m.count(extra=-1))
                    product(HID[m.slot], xop[:, m.slot, :, :, :], W1[:, X, :, :, :], True, False)
                    nc.tensor.matmul(HID[m.slot][:, :], stack[:, m.slot, :], VWst[:, :], start=False, stop=False)
                    pe.wait_ge(oh_ready, m.count())
                    nc.tensor.matmul(HID[m.slot][:, :], OH[:, m.slot, :], BT[:, :], start=False, stop=False) \
                        .then_inc(x_used, 1)
                if f.exists():
                    pe.wait_ge(stack_ready, f.count())
                    if m.exists():
                        pe.wait_ge(x1_ready, m.count())
                    nc.tensor.matmul(XV[:, :], stack[:, f.slot, :], Vst[:, :], start=True, stop=True) \
                        .then_inc(xv_ready, 1)
                if c.exists():
                    pe.wait_ge(z_ready, c.count())
                    if m.exists():
                        pe.wait_ge(t_lo, m.count())
                    transpose(TP[0], z, zT)
                if m.exists():
                    pe.wait_ge(t_lo, m.count())
                    product(HID[m.slot], ops[:, 0, :, :, :], W1[:, T_, :, :, :], False, False)
                    pe.wait_ge(h_ready, m.count())
                    pe.wait_ge(s_lo, m.count())
                    transpose(TP[1], ht, hT)
                if c.exists():
                    pe.wait_ge(z_lo, c.count())
                    if c.plus(-2).exists():
                        pe.wait_ge(o_ready, c.count(extra=-1))
                    product(OUT[c.slot], zop, W2, True, True).then_inc(w2_done, 1)
                if m.exists():
                    product(HID[m.slot], ops[:, 1, :, :, :], W1[:, S_, :, :, :], False, False)
                    pe.wait_ge(h_lo, m.count())
                    product(HID[m.slot], ops[:, 2, :, :, :], W1[:, H, :, :, :], False, True).then_inc(hid_ready, 1)

            steps(pe, step)


def kernel(**inputs):
    import concourse.bacc as bacc
    from concourse.bass_utils import run_bass_kernel_spmd

    a = {n: np.asarray(v) for n, v in inputs.items()}

    def tiled(v):
        return v.reshape(B, S // P, P, *v.shape[2:])

    def put(rows, cols, *parts):
        r = np.zeros((rows, cols), np.float32)
        for i, j, v in parts:
            r[i:i + v.shape[0], j:j + v.shape[1]] = v
        return r

    def chunks(v):
        return v.reshape(-1, P, v.shape[-1]).transpose(1, 0, 2)

    x = tiled(a["x"])
    V, W_dec, b_dec = a["L0_cond_V"], a["L0_cond_W_dec"], a["L0_cond_b_dec"]
    L1 = {n[len("L1_cond_"):]: v for n, v in a.items() if n.startswith("L1_cond_")}
    path, comp, scale = (tiled(a[n]) for n in ("itok_BxS_0_999", "itok_BxS_0_4", "mask_BxS_ik0"))
    NDEC = D * RANK
    consts = put(P, P + 1, (0, 0, np.eye(P, dtype=np.float32)),
                 (0, P, (np.arange(P) % Q).astype(np.float32)[:, None]))
    batch_eye = np.eye(B, dtype=np.float32)
    spare = (RANK, 3 * Q + RANK)
    mlps = ("mem", "noi", "res")
    arrays = {
        "x": x,
        "xT": x.reshape(B, S // P, P, KC, P).transpose(0, 1, 4, 3, 2),
        "idx": np.stack([path, comp, scale], axis=-1),
        "rows": np.stack([comp, scale], axis=1),
        "consts": consts,
        "ubc": put(P, 3, *[(q * Q, 0, b_dec[NDEC:, None]) for q in (0, 2, 3)], *[(r, 1, batch_eye) for r in spare]),
        "selrow": put(1, P, *[(0, r, np.ones((1, B), np.float32)) for r in spare]),
        "int_b1": L1["int_b1"][None], "int_b2": L1["int_b2"][None], "int_g": L1["int_g"][None],
        "int_be": L1["int_be"][None], "aw": L1["aw"][None],
        "cond": chunks(put(2 * MU, C, (0, 0, a["cond_512"].T), (MU, B, a["cond_64"].T),
                           (MU + P, 2 * B, a["fside_Bx32_0"].T))),
        "mlp_W1": chunks(put(2 * MU, D, (0, 0, L1["mem_W1"]), (MU, 0, L1["noi_W1"]), (MU + P, 0, L1["res_W1"]))),
        "svr": np.stack([np.repeat(np.stack([L1[f"{m}_{w}"] for m in mlps]), B, axis=0)
                         for w in ("b1", "b2", "g", "be")], axis=1),
        "bdec": b_dec[:NDEC].reshape(D, RANK),
        "wlast": put(MU, P, *[(0, q * Q, W_dec[:, NDEC:]) for q in (0, 2, 3)]),
        "W_dec": W_dec,
        "VT4": put(D, P, *[(0, q * Q, V.T) for q in range(4)]).reshape(KC, P, P).transpose(1, 0, 2),
        "V4": put(P, D, *[(q * Q, 0, V) for q in range(4)]),
        "BL": put(D, 3 * P, *[(0, q * Q, L1["cp_b"].T) for q in (0, 1)],
                  *[(0, P + q * Q, L1["tm_b"].T) for q in (0, 1)],
                  *[(0, 2 * P + q * Q, L1["ms_b"].T) for q in (2, 3)])
        .reshape(KC, P, 3, P).transpose(1, 2, 0, 3),
        "pw": np.concatenate([L1["pw_g"], L1["pw_b"]], axis=1),
        "ct": np.concatenate([L1["cp_g"], L1["tm_g"]], axis=1),
        "ms_g": L1["ms_g"],
        "int_W1": L1["int_W1"], "int_W2": L1["int_W2"],
    }
    arrays.update({f"{m}_W2": L1[f"{m}_W2"] for m in mlps})
    arrays = {n: np.ascontiguousarray(v) for n, v in arrays.items()}

    nc = bacc.Bacc("TRN2", target_bir_lowering=False, num_devices=1)
    d = {n: nc.dram_tensor("in_" + n, v.shape, mybir.dt.from_np(v.dtype), kind="ExternalInput").ap()
         for n, v in arrays.items()}
    out = nc.dram_tensor("out", (B, S, D), F32, kind="ExternalOutput").ap()
    build(nc, d, out)
    return run_bass_kernel_spmd(nc, [{"in_" + n: v for n, v in arrays.items()}], core_ids=[0]).results[0]["out"]
```

```python
from contextlib import ExitStack

import numpy as np
import concourse.bass as bass
from concourse import mybir

F32 = mybir.dt.float32
F32R = mybir.dt.float32r
I32 = mybir.dt.int32
ALU = mybir.AluOpType
ACT = mybir.ActivationFunctionType
AX = mybir.AxisListType

B, S, D = 2, 2048, 512
MU, NOI, RES = 256, 64, 32
RANK = 30
P = 128
KC = D // P
Q = 32
TILES = B * S // P
EPS = 1e-5
DECW = P * RANK
C = 3 * B
X, T_, S_, H = range(4)
HI, LO = 0, 1
WH, WT, WM, WN, WR, WS = range(6)
RAW = {WM: 0, WN: 1, WR: 2, WT: 3, WS: 4, WH: 5}
OFFSET_BLOCKS, OFFSETS = (WT, WS, WH), (5, 3, 5)
OFFSET_QUADRANTS = (0, 1), (2, 3), (0, 1)
NSTAGE = 6
PAIRS = 2 * KC
HALF = DECW // 2
BANK = HALF // 4
FIRST, LAST = 3, TILES - 3


class Tile:

    def __init__(self, s, i=None):
        self.s, self.i, self.slot, self.batch = s, i, s % 2, s % 2

    def plus(self, k):
        return Tile(self.s + k, self.i)

    def count(self, each=1, extra=1):
        v = (self.s + extra) * each
        return v if self.i is None else self.i * (2 * each) + v

    def slot_count(self, each):
        v = (self.s // 2 + 1) * each
        return v if self.i is None else self.i * each + v

    def pair(self):
        return self.s // 2 if self.i is None else self.i + self.s // 2

    def exists(self):
        return self.i is not None or 0 <= self.s < TILES


def is_first(t):
    return t.i is None and t.s == 0


def steps(eng, emit):
    for n in range(-2, FIRST):
        emit(Tile(n))
    with eng.Fori(0, (LAST - FIRST) // 2) as i:
        emit(Tile(FIRST, i))
        emit(Tile(FIRST + 1, i))
    for n in range(LAST, TILES + 1):
        emit(Tile(n))


def build(nc, d, out):
    with ExitStack() as ctx:
        def sem(name):
            return ctx.enter_context(nc.semaphore(name))

        def sem2(name):
            return [sem(f"{name}{i}") for i in range(2)]

        cursor = [(nc.sbuf_base + 31) // 32 * 32]

        def sb(name, shape, dt=F32):
            t = nc.alloc_sbuf_tensor_at(name, shape, dt, offset=cursor[0])
            cursor[0] += (int(np.prod(shape[1:])) * 4 + 31) // 32 * 32
            return t

        def back_to(mark):
            end, cursor[0] = cursor[0], mark
            return end

        W1 = sb("W1", [P, 4, 2, KC, D], F32R)
        W2 = sb("W2", [P, 2, KC, D], F32R)
        Ust = sb("Ust", [P, B, KC, P], F32R)
        Vst = sb("Vst", [P, D], F32R)
        VWst = sb("VWst", [P, D], F32R)
        BT = sb("BT", [P, D], F32R)
        ub = sb("ub", [P, B])
        consts = sb("consts", [P, P + 1])
        ident, inquad = consts[:, 0:P], consts[:, P:P + 1]

        at_lm = cursor[0]
        LM = sb("LM", [P, 3, KC, P])
        at_raw = cursor[0]
        raw = sb("raw", [P, 6, KC, D])
        BL = sb("BL", [P, 3, KC, P])
        selr = sb("selr", [1, P + D])
        aw = sb("aw", [P, 6])
        wexp = sb("wexp", [P, 6])
        wsm = sb("wsm", [P, 6])
        sc = sb("sc", [P, 3])
        svr = raw[0:C, RAW[WS], :, :]
        hid, vec = (raw[0:C, RAW[WH], c, :] for c in range(2))

        at_top = cursor[0]
        stage = sb("stage", [P, NSTAGE - 2, KC * D])
        V4 = sb("V4", [P, D])
        bt = sb("bt", [P, KC, sum(OFFSETS)])
        wlast = sb("wlast", [P, 2, P])
        hidT = sb("hidT", [P, 3, KC, C])
        at_ur = cursor[0]
        Ur = sb("Ur", [P, DECW])
        Uf = sb("Uf", [P, KC, 2 * B, RANK])
        cond = sb("cond", [P, 4, C])
        condr = sb("condr", [P, 2, 2 * B], F32R)
        bdec = sb("bdec", [P, KC, RANK])
        ubc = sb("ubc", [P, 3])
        vst = sb("vst", [C, 6])
        vmv = sb("vmv", [C, 2])
        vrs = sb("vrs", [C, 3])

        back_to(at_top)
        xT = sb("xT", [P, 2, KC, P])
        x0 = sb("x0", [P, 2, D])
        idx = sb("idx", [P, 2, 3], I32)
        idxrep = sb("idxrep", [P, 2, P], I32)
        xop = sb("xop", [P, 2, 2, KC, P], F32R)
        OH = sb("OH", [P, 2, P], F32R)
        mhalf = sb("mhalf", [P, 1])
        ctt = sb("ctt", [P, 2, 2 * D])
        sgt = sb("sgt", [P, 2, D])
        pwt = sb("pwt", [P, 2, 2 * D])
        assert cursor[0] - 2 * D * 4 <= at_ur
        stack = sb("stack", [P, 2, P], F32R)
        inner = sb("inner", [P, P])
        x1 = sb("x1", [P, 2, D])
        xhat = sb("xhat", [P, D])
        tt = sb("tt", [P, D])
        st = sb("st", [P, D])
        h1 = sb("h1", [P, D])
        ht = sb("ht", [P, D])
        bn = sb("bn", [P, 3, 6])
        mv = sb("mv", [P, 3, 2])
        ve = sb("ve", [P, 3])
        rs = sb("rs", [P, 3])
        back_to(at_lm)
        xb = sb("xb", [P, 2, D])
        bebc = sb("bebc", [P, D])
        assert cursor[0] == at_raw
        ops = sb("ops", [P, 3, 2, KC, P], F32R)
        zop = sb("zop", [P, 2, KC, P], F32R)
        z = sb("z", [P, D])
        b2bc, gbc = sb("b2bc", [P, D]), sb("gbc", [P, D])
        assert cursor[0] <= at_raw + 3 * KC * D * 4
        back_to(at_raw + 3 * KC * D * 4)
        w2raw = sb("w2raw", [P, KC, D])
        back_to(at_raw + 3 * KC * D * 4)
        o = sb("o", [P, D])
        u = sb("u", [P, D])
        y = sb("y", [P, 2, D])

        bank = [nc.alloc_psum_tensor(f"bank{i}", [P, 512], F32) for i in range(8)]
        pM, pT, pVW, pBT = bank[4:8]
        pU = bank[0:2] + bank[6:8] + bank[2:4]
        HIDT, VECT, ULAST = pT[:, 0:KC * C], pT[:, 64:64 + KC * C], pT[:, 128:128 + B]
        XU, XV = bank[0:2]
        TP, HID, OUT = bank[2:4], bank[4:6], bank[6:8]

        cond_in, mlp_in, sel_in, aw_in = sem("cond_in"), sem("mlp_rows_in"), sem("sel_in"), sem("aw_in")
        consts_in, late_in = sem("consts_in"), sem("late_in")
        raw_in = [sem(f"raw_in{i}") for i in range(6)]
        stage_in = [sem(f"stage_in{i}") for i in range(NSTAGE)]
        mlp_used = sem("mlp_used")
        condr_ready = sem("condr_ready")
        dec_hi, dec_lo = sem("dec_hi"), sem("dec_lo")
        half_used = sem("half_used")
        u_bank = sem("u_bank")
        u_row = [sem("u_row_act"), sem("u_row_dve")]
        u_in, u_in_act = [sem(f"u_in{c}") for c in range(KC)], sem("u_in_act")
        dve, pool_prep = sem("dve_prep"), sem("pool_prep")
        max_ready, exp_ready, w_ready = sem("max_ready"), sem("exp_ready"), sem("w_ready")
        pre_ready, silu_ready, hidT_sum, hidT_ready = (sem("pre_ready"), sem("silu_ready"), sem("hidT_sum"),
                                                       sem("hidT_ready"))
        var_ready, rst_ready = sem("var_ready"), sem("rst_ready")
        vec_ready, vecT_sum, lm_ready, bl_ready = sem("vec_ready"), sem("vecT_sum"), sem("lm_ready"), sem("bl_ready")
        zeroed, ulast_ready = sem("zeroed"), sem("ulast_ready")
        vst_ready, ust_ready = sem("vst_ready"), sem("ust_ready")
        w2_in, w2_hi, w2_lo = sem("w2_in"), sem("w2_hi"), sem("w2_lo")
        vw_m, vw_ready, bt_sum = sem("vw_m"), sem("vw_ready"), sem("bt_sum")
        wx_m, wx_ready, wx_hi, wx_lo = sem("wx_m"), sem("wx_ready"), sem("wx_hi"), sem("wx_lo")
        vwst_ready, bt_ready = sem("vwst_ready"), sem("bt_ready")
        t_scaled, t_block_lo = sem("t_scaled"), sem("t_block_lo")
        w1_hi, w1_lo = sem("w1_hi"), sem("w1_lo")

        xT_in, x0_in, idx_in, rep_in = sem2("xT_in"), sem2("x0_in"), sem2("idx_in"), sem2("rep_in")
        pw_in, ct_in, sg_in, stored = sem2("pw_in"), sem2("ct_in"), sem2("sg_in"), sem2("stored")
        x_hi, x_lo, x_used, oh_ready = sem("x_hi"), sem("x_lo"), sem("x_used"), sem("oh_ready")
        inner_part, inner_ready = sem("inner_part"), sem("inner_ready")
        xu_ready, stack_part, stack_ready, xv_ready = sem("xu_ready"), sem("stack_part"), sem("stack_ready"), sem("xv_ready")
        x1_ready, bn_done, mv1_ready, r1_ready = sem("x1_ready"), sem("bn_done"), sem("mv1_ready"), sem("r1_ready")
        xhat_ready, t_ready, s_ready, h1_part, h1_ready = (sem("xhat_ready"), sem("t_ready"), sem("s_ready"),
                                                           sem("h1_part"), sem("h1_ready"))
        mv2_ready, r2_ready, hn_ready, h_ready = sem("mv2_ready"), sem("r2_ready"), sem("hn_ready"), sem("h_ready")
        tT, sT, hT, zT = sem("tT"), sem("sT"), sem("hT"), sem("zT")
        t_hi, s_hi, h_hi, z_hi = sem("t_hi"), sem("s_hi"), sem("h_hi"), sem("z_hi")
        t_lo, s_lo, h_lo, z_lo = sem("t_lo"), sem("s_lo"), sem("h_lo"), sem("z_lo")
        hid_ready, z_ready, w2_done, o_ready = sem("hid_done"), sem("z_ready"), sem("w2_done"), sem("o_ready")
        mv3_ready, r3_ready, xb_ready, u_ready, y_ready = (sem("mv3_ready"), sem("r3_ready"), sem("xb_ready"),
                                                           sem("u_done"), sem("y_ready"))
        pool_part, mhalf_ready = sem("pool_part"), sem("mhalf_ready")
        rows_in, bebc_in = sem("rows_in"), sem("bebc_in")

        def load(eng, got, *pairs):
            for dst, src in pairs:
                eng.dma_start(dst, src).then_inc(got, 16)

        DEC = [("dec", j) for j in range(2 * PAIRS)]
        MLP2 = [("mlp2", m) for m in range(3)]
        ring = [("mlp1", 0)] + DEC[:4] + MLP2 + DEC[4:]
        slot = {item: i % NSTAGE for i, item in enumerate(ring)}
        arrived = {item: 16 * (i // NSTAGE + 1) for i, item in enumerate(ring)}

        def source(item):
            kind, j = item
            if kind == "mlp1":
                return d["mlp_W1"]
            if kind == "mlp2":
                return d[("mem_W2", "noi_W2", "res_W2")[j]].rearrange("(c p) n -> p c n", p=P)
            return d["W_dec"][j % 2 * P:(j % 2 + 1) * P, j // 2 * HALF:(j // 2 + 1) * HALF]

        def staged(item):
            if slot[item] < NSTAGE - 2:
                s = stage[:, slot[item], :]
            else:
                s = block_of((WR, WT)[slot[item] - NSTAGE + 2]).rearrange("p c n -> p (c n)")
            return s[:, 0:HALF] if item[0] == "dec" else s.rearrange("p (c n) -> p c n", n=D)

        def left_stage(item):
            kind, j = item
            return {"mlp1": (mlp_used, 1), "mlp2": (mlp_used, 2 + j), "dec": (dec_lo, j + 1)}[kind]

        def parts_used(j):
            return (u_bank, 4 * (j // 2 + 1)) if j % 2 else (half_used, j // 2 + 1)

        def dec_part(j, part):
            return W1[:, j % 4, part, :, :].rearrange("p c n -> p (c n)")[:, 0:HALF]

        def block_of(src):
            return raw[:, RAW[src], :, :]

        def load_block(sp, src):
            load(sp, raw_in[src], (block_of(src), d["int_W1"][src * D:(src + 1) * D, :].rearrange(
                "(c p) n -> p c n", p=P)))

        def u_bank_of(pair, g):
            return pU[(4 * pair + g) % len(pU)][0:2 * B, 0:BANK]

        def evacuate(copy, pair, g, done):
            c, h = divmod(pair, 2)
            col = h * HALF + g * BANK
            copy(Ur[c * Q:c * Q + 2 * B, col:col + BANK], u_bank_of(pair, g)).then_inc(done, 1)

        def to_features(eng, got, c, rows):
            eng.wait_ge(u_row[0], 6 * (c + 1))
            eng.wait_ge(u_row[1], 2 * (c + 1))
            load(eng, got, *[(Uf[:, c, j, :], Ur[c * Q + j:c * Q + j + 1, :].rearrange("o (p r) -> o p r", r=RANK))
                                 for j in rows])

        def features(compute, c, link):
            link(compute.tensor_tensor(Uf[:, c, 0:B, :], Uf[:, c, 0:B, :], Uf[:, c, B:2 * B, :], ALU.add))
            for b in range(B):
                last = compute.tensor_tensor(Uf[:, c, b, :], Uf[:, c, b, :], bdec[:, c, :], ALU.add)
            link(last)
            for q in (2, 3, 0):
                last = compute.tensor_copy(Ust[:, :, c, q * Q:q * Q + RANK], Uf[:, c, 0:B, :])
            link(last)
            compute.tensor_tensor(Ust[:, :, c, Q:Q + RANK], Uf[:, c, 0:B, :],
                                  Ust[:, :, c, 0:RANK].bitcast(F32), ALU.subtract).then_inc(ust_ready, 1)

        block = ctx.enter_context(nc.Block())
        outv = out.rearrange("b (j p) n -> b j p n", p=P)

        @block.sync
        def _(sp):
            for i, item in enumerate(ring):
                if i >= NSTAGE:
                    sp.wait_ge(*left_stage(ring[i - NSTAGE]))
                load(sp, stage_in[slot[item]], (staged(item), source(item)))
            for src in (WM, WN, WR):
                if src == WR:
                    sp.wait_ge(dec_lo, 2 * PAIRS)
                load_block(sp, src)

            def after_second_loads():
                sp.wait_ge(u_in_act, 16 * B)
                sp.wait_ge(vecT_sum, 1)
                for src in (WT, WS, WH):
                    load_block(sp, src)
                sp.wait_ge(vw_ready, 1)
                load(sp, bebc_in, (bebc[:, :], d["int_be"].to_broadcast([P, D])))
                sp.wait_ge(wx_lo, 1)
                load(sp, rows_in, (b2bc[:, :], d["int_b2"].to_broadcast([P, D])),
                     (gbc[:, :], d["int_g"].to_broadcast([P, D])))

            def after_third_loads():
                sp.wait_ge(bt_sum, 1)
                sp.wait_ge(t_block_lo, 1)
                load(sp, w2_in, (w2raw[:, :, :], d["int_W2"].rearrange("(c p) n -> p c n", p=P)))

            def step(n):
                a = n.plus(2)
                if n.s == -2:
                    sp.wait_ge(dec_lo, 2 * PAIRS)
                if a.exists():
                    s, old = a.slot, a.plus(-2)
                    if old.exists():
                        sp.wait_ge(x_lo, old.count())
                    sp.dma_start(xT[:, s, :, :], d["xT"][s, bass.ds(a.pair(), 1), :, :, :].rearrange(
                        "o p c t -> (o p) c t")).then_inc(xT_in[s], 16)
                    if old.exists():
                        sp.wait_ge(x1_ready, old.count())
                    sp.dma_start(x0[:, s, :], d["x"][s, bass.ds(a.pair(), 1), :, :].rearrange("o p n -> (o p) n")) \
                      .then_inc(x0_in[s], 16)
                    if old.exists():
                        sp.wait_ge(sg_in[s], old.slot_count(16))
                        sp.wait_ge(ct_in[s], old.slot_count(16))
                        sp.wait_ge(pw_in[s], old.slot_count(16))
                    sp.dma_start(idx[:, s, :], d["idx"][s, bass.ds(a.pair(), 1), :, :].rearrange("o p n -> (o p) n")) \
                      .then_inc(idx_in[s], 16)
                    if old.exists():
                        sp.wait_ge(oh_ready, old.count())
                    for half in range(2):
                        sp.dma_start(idxrep[half * P // 2:(half + 1) * P // 2, s, :],
                                     d["rows"][s, half, bass.ds(a.pair(), 1), :].to_broadcast([P // 2, P])) \
                          .then_inc(rep_in[s], 16)
                if n.s == -1:
                    after_second_loads()
                if is_first(n):
                    after_third_loads()
                if n.plus(-2).exists():
                    store(n.plus(-2))

            def store(c):
                sp.wait_ge(y_ready, c.count())
                sp.dma_start(outv[c.batch, bass.ds(c.pair(), 1), :, :].rearrange("o p n -> (o p) n"),
                             y[:, c.slot, :]).then_inc(stored[c.slot], 16)

            steps(sp, step)
            store(Tile(TILES - 1))
            for s in range(2):
                sp.wait_ge(stored[s], 16 * TILES // 2)

        @block.scalar
        def _(act):
            load(act, cond_in, (cond[:, :, :], d["cond"]))
            load(act, mlp_in, (svr, d["svr"]))
            load(act, aw_in, (aw[:, :], d["aw"].to_broadcast([P, 6])))
            load(act, consts_in, (consts[:, :], d["consts"][:, 0:P + 1]))
            load(act, sel_in, (wlast[:, :, :], d["wlast"].rearrange("(c p) r -> p c r", p=P)), (ubc[:, :], d["ubc"]),
                 (selr[0:1, 0:P], d["selrow"]), (selr[0:1, P:P + D], d["int_b1"]),
                 (bdec[:, :, :], d["bdec"].rearrange("(c p) r -> p c r", p=P)))
            load(act, late_in, (V4[:, :], d["V4"]), (bt[:, :, :], d["bt"]), (LM[:, 0, :, :], d["VT4"]))

            def dec_high(j):
                act.wait_ge(stage_in[slot[DEC[j]]], arrived[DEC[j]])
                if j >= 4:
                    act.wait_ge(*parts_used(j - 4))
                nc.scalar.activation(dec_part(j, HI), staged(DEC[j]), ACT.Copy).then_inc(dec_hi, 1)

            def rows_of(pair):
                for g in range(3):
                    act.wait_ge(u_bank, 4 * pair + g + 1)
                    evacuate(lambda dst, src: nc.scalar.activation(dst, src, ACT.Copy), pair, g, u_row[0])

            for j in range(2 * PAIRS):
                dec_high(j)
                if j == 0:
                    act.wait_ge(max_ready, 1)
                    nc.scalar.activation(wexp[:, :], aw[:, :], ACT.Exp, bias=sc[:, 0:1],
                                         accum_out=sc[:, 1:2]).then_inc(exp_ready, 1)
                    act.wait_ge(pre_ready, 1)
                    nc.scalar.activation(hid, hid, ACT.Silu, bias=0.0).then_inc(silu_ready, 1)
                if j == 2:
                    rows_of(0)
                if j % 2 == 1 and j > 3:
                    rows_of(j // 2 - 1)
            rows_of(PAIRS - 1)
            to_features(act, u_in_act, KC - 1, range(B, 2 * B))

            def high_part(blk, src):
                act.wait_ge(raw_in[src], 16)
                nc.scalar.activation(W1[:, blk, HI, :, :], block_of(src), ACT.Copy,
                                     scale=wsm[:, src:src + 1]).then_inc(w1_hi, 1)

            def after_second_split():
                act.wait_ge(w_ready, 1)
                act.wait_ge(vw_m, 1)
                nc.scalar.activation(block_of(WM), block_of(WM), ACT.Copy, scale=wsm[:, WM:WM + 1]).then_inc(wx_m, 1)
                act.wait_ge(raw_in[WT], 16)
                nc.scalar.activation(block_of(WT), block_of(WT), ACT.Copy, scale=wsm[:, WT:WT + 1]) \
                    .then_inc(t_scaled, 1)
                act.wait_ge(t_scaled, 1)
                nc.scalar.activation(W1[:, T_, HI, :, :], block_of(WT), ACT.Copy).then_inc(w1_hi, 1)
                act.wait_ge(wx_ready, 2)
                nc.scalar.activation(W1[:, X, HI, :, :], block_of(WM), ACT.Copy).then_inc(wx_hi, 1)
                high_part(S_, WS)
                high_part(H, WH)

            def split_w2():
                act.wait_ge(w2_in, 16)
                nc.scalar.activation(W2[:, HI, :, :], w2raw[:, :, :], ACT.Copy).then_inc(w2_hi, 1)


            def split_hi(dst, bank, have, t, done):
                act.wait_ge(have, t.count())
                nc.scalar.activation(dst.rearrange("p c t -> p (c t)"), bank[:, :], ACT.Copy).then_inc(done, 1)

            def step(n):
                a, m, c = n.plus(2), n, n.plus(-1)
                if is_first(m):
                    act.wait_ge(wx_lo, 1)
                if m.exists():
                    split_hi(ops[:, 0, HI, :, :], TP[0], tT, m, t_hi)
                    split_hi(ops[:, 1, HI, :, :], TP[1], sT, m, s_hi)
                if a.exists():
                    s, old = a.slot, a.plus(-2)
                    act.wait_ge(xT_in[s], a.slot_count(16))
                    if old.exists():
                        act.wait_ge(x_used, old.count())
                    nc.scalar.activation(xop[:, s, HI, :, :], xT[:, s, :, :], ACT.Copy).then_inc(x_hi, 1)
                if n.s == -1:
                    after_second_split()
                if is_first(m):
                    split_w2()
                if c.exists():
                    split_hi(zop[:, HI, :, :], TP[0], zT, c, z_hi)
                if m.exists():
                    split_hi(ops[:, 2, HI, :, :], TP[1], hT, m, h_hi)
                    act.wait_ge(hid_ready, m.count())
                    nc.scalar.activation(z[:, :], HID[m.slot][:, :], ACT.Silu, bias=0.0).then_inc(z_ready, 1)

            steps(act, step)

        @block.tensor
        def _(pe):
            def wait_for(item):
                pe.wait_ge(stage_in[slot[item]], arrived[item])

            def decode(j):
                pair, m = divmod(j, 2)
                pe.wait_ge(dec_lo, j + 1)
                for g in range(4):
                    before = divmod(4 * pair + g - len(pU), 4)
                    if m == 0 and before[0] >= 0:
                        pe.wait_ge(u_row[before[1] // 3],
                                   before[0] + 1 if before[1] == 3 else 3 * before[0] + before[1] + 1)
                    for part in (HI, LO):
                        last = nc.tensor.matmul(u_bank_of(pair, g), condr[:, m, :],
                                                dec_part(j, part)[:, g * BANK:(g + 1) * BANK],
                                                start=(m == 0 and part == HI), stop=(m == 1 and part == LO))
                    if m == 1:
                        last.then_inc(u_bank, 1)
                if m == 0:
                    last.then_inc(half_used, 1)

            pe.wait_ge(cond_in, 16)
            wait_for(("mlp1", 0))
            for c in range(4):
                last = nc.tensor.matmul(pM[0:C, :], cond[:, c, :], staged(("mlp1", 0))[:, c, :],
                                        start=(c == 0), stop=(c == 3))
            last.then_inc(mlp_used, 1)
            pe.wait_ge(condr_ready, 2)
            decode(0)
            pe.wait_ge(silu_ready, 1)
            pe.wait_ge(consts_in, 16)
            for c in range(KC):
                last = nc.tensor.transpose(HIDT[:, c * C:(c + 1) * C], hid[:, c * P:(c + 1) * P], ident[0:C, 0:C])
            last.then_inc(hidT_sum, 1)
            decode(1)
            decode(2)
            decode(3)
            pe.wait_ge(hidT_ready, 3)
            pe.wait_ge(sel_in, 16 * 5)
            for m in range(2):
                last = nc.tensor.matmul(ULAST, wlast[:, m, :], cond[:, m, 0:B], start=(m == 0), stop=(m == 1))
            last.then_inc(ulast_ready, 1)
            for m in range(3):
                wait_for(MLP2[m])
                for c in range(KC):
                    last = nc.tensor.matmul(pM[0:C, :], hidT[:, m, c, :], staged(MLP2[m])[:, c, :],
                                            start=(m == 0 and c == 0), stop=(m == 2 and c == KC - 1))
                last.then_inc(mlp_used, 1)
            for j in range(4, 10):
                decode(j)
            pe.wait_ge(vec_ready, 1)
            for c in range(KC):
                last = nc.tensor.transpose(VECT[:, c * C:(c + 1) * C], vec[:, c * P:(c + 1) * P], ident[0:C, 0:C])
            last.then_inc(vecT_sum, 1)
            for j in range(10, 2 * PAIRS):
                decode(j)
            pe.wait_ge(lm_ready, 2)
            pe.wait_ge(u_row[0], 3 * (PAIRS - 1))
            pe.wait_ge(u_row[1], PAIRS - 1)
            nc.tensor.matmul(pVW[:, :], selr[0:1, 0:P], selr[0:1, P:P + D], start=True, stop=False)
            for m, (blk, done) in enumerate(((WM, vw_m), (WN, None), (WR, vw_ready))):
                pe.wait_ge(raw_in[blk], 16)
                for c in range(KC):
                    last = nc.tensor.matmul(pVW[:, :], LM[:, m, c, :], block_of(blk)[:, c, :],
                                            start=False, stop=(m == 2 and c == KC - 1))
                if done is not None:
                    last.then_inc(done, 1)

            def after_first_front():
                pe.wait_ge(bl_ready, 3)
                for t, blk in enumerate(OFFSET_BLOCKS):
                    if blk == WT:
                        pe.wait_ge(t_scaled, 1)
                    else:
                        pe.wait_ge(raw_in[blk], 16)
                    for c in range(KC):
                        last = nc.tensor.matmul(pBT[:, :], BL[:, t, c, :], block_of(blk)[:, c, :],
                                                start=(t == 0 and c == 0), stop=(t == 2 and c == KC - 1))
                last.then_inc(bt_sum, 1)

            def transpose(dst, src, done):
                for c in range(KC):
                    last = nc.tensor.transpose(dst[:, c * P:(c + 1) * P], src[:, c * P:(c + 1) * P], ident)
                last.then_inc(done, 1)

            def product(bank, op, w, start, stop):
                for c in range(KC):
                    nc.tensor.matmul(bank[:, :], op[:, HI, c, :], w[:, HI, c, :], start=start and c == 0, stop=False)
                    nc.tensor.matmul(bank[:, :], op[:, HI, c, :], w[:, LO, c, :], start=False, stop=False)
                    last = nc.tensor.matmul(bank[:, :], op[:, LO, c, :], w[:, HI, c, :], start=False,
                                            stop=stop and c == KC - 1)
                return last

            def step(n):
                f, m, c = n.plus(1), n, n.plus(-1)
                if m.exists():
                    pe.wait_ge(t_ready, m.count())
                    if m.plus(-2).exists():
                        pe.wait_ge(z_lo, m.count(extra=-1))
                    transpose(TP[0], tt, tT)
                    pe.wait_ge(s_ready, m.count())
                    if m.plus(-1).exists():
                        pe.wait_ge(h_lo, m.count(extra=0))
                    transpose(TP[1], st, sT)
                if f.exists():
                    pe.wait_ge(x_lo, f.count())
                    if is_first(f):
                        pe.wait_ge(ust_ready, KC)
                    if m.exists():
                        pe.wait_ge(stack_ready, m.count())
                    for q in range(KC):
                        last = nc.tensor.matmul(XU[:, 0:2 * P], Ust[:, f.batch, q, :], xop[:, f.slot, :, q, :],
                                                start=(q == 0), stop=(q == KC - 1))
                    last.then_inc(xu_ready, 1)
                if m.exists():
                    if m.plus(-2).exists():
                        pe.wait_ge(z_ready, m.count(extra=-1))
                    if is_first(m):
                        pe.wait_ge(wx_lo, 1)
                    product(HID[m.slot], xop[:, m.slot, :, :, :], W1[:, X, :, :, :], True, False)
                    if is_first(m):
                        pe.wait_ge(vwst_ready, 1)
                        pe.wait_ge(bt_ready, 1)
                    nc.tensor.matmul(HID[m.slot][:, :], stack[:, m.slot, :], VWst[:, :], start=False, stop=False)
                    pe.wait_ge(oh_ready, m.count())
                    nc.tensor.matmul(HID[m.slot][:, :], OH[:, m.slot, :], BT[:, :], start=False, stop=False) \
                        .then_inc(x_used, 1)
                if f.exists():
                    pe.wait_ge(stack_ready, f.count())
                    if is_first(f):
                        pe.wait_ge(vst_ready, 1)
                    if m.exists():
                        pe.wait_ge(x1_ready, m.count())
                    nc.tensor.matmul(XV[:, :], stack[:, f.slot, :], Vst[:, :], start=True, stop=True) \
                        .then_inc(xv_ready, 1)
                if is_first(f):
                    after_first_front()
                if c.exists():
                    pe.wait_ge(z_ready, c.count())
                    if m.exists():
                        pe.wait_ge(t_lo, m.count())
                    transpose(TP[0], z, zT)
                if m.exists():
                    pe.wait_ge(t_lo, m.count())
                    if is_first(m):
                        pe.wait_ge(t_block_lo, 1)
                    product(HID[m.slot], ops[:, 0, :, :, :], W1[:, T_, :, :, :], False, False)
                    pe.wait_ge(h_ready, m.count())
                    pe.wait_ge(s_lo, m.count())
                    transpose(TP[1], ht, hT)
                if c.exists():
                    pe.wait_ge(z_lo, c.count())
                    if c.plus(-2).exists():
                        pe.wait_ge(o_ready, c.count(extra=-1))
                    if is_first(c):
                        pe.wait_ge(w2_lo, 1)
                    product(OUT[c.slot], zop, W2, True, True).then_inc(w2_done, 1)
                if m.exists():
                    if is_first(m):
                        pe.wait_ge(w1_lo, 1)
                    product(HID[m.slot], ops[:, 1, :, :, :], W1[:, S_, :, :, :], False, False)
                    pe.wait_ge(h_lo, m.count())
                    if is_first(m):
                        pe.wait_ge(w1_lo, 2)
                    product(HID[m.slot], ops[:, 2, :, :, :], W1[:, H, :, :, :], False, True).then_inc(hid_ready, 1)

            steps(pe, step)

        @block.gpsimd
        def _(pool):
            nc.gpsimd.memset(hidT[:, :, :, :], 0.0).then_inc(zeroed, 1)
            nc.gpsimd.memset(vrs[:, 1:2], -0.5).then_inc(pool_prep, 1)
            nc.gpsimd.memset(BL[:, :, :, :], 0.0).then_inc(zeroed, 1)
            nc.gpsimd.memset(Ust[:, :, :, :].bitcast(F32), 0.0).then_inc(zeroed, 1)
            pool.wait_ge(pool_prep, 1)
            pool.wait_ge(var_ready, 1)
            nc.gpsimd.tensor_tensor(vrs[:, 2:3], vrs[:, 0:1], vrs[:, 1:2], ALU.pow).then_inc(rst_ready, 1)
            links = [1]

            def link(ins):
                links[0] += 1
                ins.then_inc(pool_prep, 1)
                pool.wait_ge(pool_prep, links[0])

            pool.wait_ge(sel_in, 16 * 5)
            for c in range(KC):
                to_features(pool, u_in[c], c, range(2 * B if c < KC - 1 else B))
                if c > 0:
                    pool.wait_ge(u_in[c - 1], 16 * 2 * B)
                    features(nc.gpsimd, c - 1, link)
            pool.wait_ge(dec_lo, 2 * PAIRS)

            def low_part_of_t():
                pool.wait_ge(w1_hi, 1)
                nc.gpsimd.tensor_tensor(W1[:, T_, LO, :, :], block_of(WT), W1[:, T_, HI, :, :].bitcast(F32),
                                        ALU.subtract).then_inc(t_block_lo, 1)

            nc.gpsimd.memset(mhalf[:, :], -0.5).then_inc(mhalf_ready, 1)

            def rstd(which, t, have, done):
                pool.wait_ge(have, t.count())
                pool.nop(nofuse=True)
                nc.gpsimd.tensor_scalar(ve[:, which:which + 1], mv[:, which, 1:2], EPS, 1.0, ALU.add, ALU.mult) \
                    .then_inc(pool_part, 1)
                parts[0] += 1
                pool.wait_ge(pool_part, part_count(t))
                nc.gpsimd.tensor_tensor(rs[:, which:which + 1], ve[:, which:which + 1], mhalf[:, :],
                                        ALU.pow).then_inc(done, 1)

            parts = [0]
            base = [0, None]

            def part_count(t):
                return parts[0] if base[1] is None else base[1] * base[0] + parts[0]

            def step(n):
                a, f, c = n.plus(2), n.plus(1), n.plus(-1)
                if n.s == -1:
                    pool.wait_ge(ust_ready, KC)
                if a.exists():
                    s, old = a.slot, a.plus(-2)
                    pool.wait_ge(idx_in[s], a.slot_count(16))
                    if old.exists():
                        pool.wait_ge(h_ready, old.count())
                    pool.nop(nofuse=True)
                    for dst, table, col, got in ((ctt[:, s, :], d["ct"], 1, ct_in), (sgt[:, s, :], d["ms_g"], 2, sg_in),
                                                 (pwt[:, s, :], d["pw"], 0, pw_in)):
                        pool.indirect_dma_start(out=dst, out_offset=None, in_=table,
                                                in_offset=bass.IndirectOffsetOnAxis(ap=idx[:, s, col:col + 1], axis=0)) \
                            .then_inc(got[s], 16)
                if f.exists():
                    s = f.slot
                    rstd(0, f, mv1_ready, r1_ready)
                    pool.wait_ge(xhat_ready, f.count())
                    pool.wait_ge(pw_in[s], f.slot_count(16))
                    if f.plus(-1).exists():
                        pool.wait_ge(hn_ready, f.count(extra=0))
                    nc.gpsimd.tensor_tensor(h1[:, :], xhat[:, :], pwt[:, s, 0:D], ALU.mult).then_inc(h1_part, 1)
                    pool.wait_ge(h1_part, f.count())
                    nc.gpsimd.tensor_tensor(h1[:, :], h1[:, :], pwt[:, s, D:2 * D], ALU.add).then_inc(h1_ready, 1)
                if a.exists():
                    s = a.slot
                    pool.wait_ge(x_hi, a.count())
                    nc.gpsimd.tensor_tensor(xop[:, s, LO, :, :], xT[:, s, :, :], xop[:, s, HI, :, :].bitcast(F32),
                                            ALU.subtract).then_inc(x_lo, 1)
                if is_first(f):
                    low_part_of_t()
                if f.exists():
                    rstd(1, f, mv2_ready, r2_ready)
                if c.exists():
                    rstd(2, c, mv3_ready, r3_ready)
                if f.exists():
                    s = f.slot
                    if f.plus(-2).exists():
                        pool.wait_ge(y_ready, f.count(extra=-1))
                    if is_first(f):
                        pool.wait_ge(bebc_in, 16)
                    pool.wait_ge(x1_ready, f.count())
                    nc.gpsimd.tensor_tensor(xb[:, s, :], x1[:, s, :], bebc[:, :], ALU.add).then_inc(xb_ready, 1)

            pool.wait_ge(mhalf_ready, 1)
            for n in range(-2, FIRST):
                step(Tile(n))
            with pool.Fori(0, (LAST - FIRST) // 2) as i:
                before = parts[0]
                base[:] = [6, i]
                step(Tile(FIRST, i))
                step(Tile(FIRST + 1, i))
                assert parts[0] - before == 6
            parts[0] = before + 6 * ((LAST - FIRST) // 2)
            base[1] = None
            for n in range(LAST, TILES + 1):
                step(Tile(n))

        @block.vector
        def _(v):
            seen = [0]

            def link(ins):
                seen[0] += 1
                ins.then_inc(dve, 1)
                v.wait_ge(dve, seen[0])

            def dec_low(*items):
                for j in items:
                    v.wait_ge(dec_hi, j + 1)
                    nc.vector.tensor_tensor(dec_part(j, LO), staged(DEC[j]), dec_part(j, HI).bitcast(F32),
                                            ALU.subtract).then_inc(dec_lo, 1)
                    if j % 2 == 0 and j > 0:
                        fourth_bank(j // 2 - 1)

            def fourth_bank(pair):
                v.wait_ge(u_bank, 4 * (pair + 1))
                evacuate(nc.vector.tensor_copy, pair, 3, u_row[1])

            v.wait_ge(cond_in, 16)
            nc.vector.tensor_copy(condr[:, :, 0:B], cond[:, 0:2, 0:B]).then_inc(condr_ready, 1)
            v.wait_ge(condr_ready, 1)
            nc.vector.tensor_tensor(condr[:, :, B:2 * B], cond[:, 0:2, 0:B], condr[:, :, 0:B].bitcast(F32),
                                    ALU.subtract).then_inc(condr_ready, 1)
            v.wait_ge(aw_in, 16)
            nc.vector.tensor_reduce(sc[:, 0:1], aw[:, :], axis=AX.X, op=ALU.max, negate=True).then_inc(max_ready, 1)
            dec_low(0)
            v.wait_ge(mlp_in, 16)
            v.wait_ge(mlp_used, 1)
            nc.vector.tensor_tensor(hid, pM[0:C, :], svr[:, 0, :], ALU.add).then_inc(pre_ready, 1)
            v.wait_ge(exp_ready, 1)
            link(nc.vector.reciprocal(sc[:, 2:3], sc[:, 1:2]))
            nc.vector.tensor_scalar(wsm[:, :], wexp[:, :], sc[:, 2:3], None, ALU.mult).then_inc(w_ready, 1)
            v.wait_ge(zeroed, 3)
            v.wait_ge(hidT_sum, 1)
            for m in range(3):
                nc.vector.tensor_copy(hidT[:, m, :, m * B:(m + 1) * B],
                                      HIDT.rearrange("p (c j) -> p c j", j=C)[:, :, m * B:(m + 1) * B]) \
                    .then_inc(hidT_ready, 1)
            dec_low(1, 2, 3)
            v.wait_ge(late_in, 16 * 3)
            link(nc.vector.tensor_copy(Vst[:, :], V4[:, :]))
            nc.vector.tensor_tensor(Vst[3 * Q:P, :], V4[3 * Q:P, :], Vst[3 * Q:P, :].bitcast(F32),
                                    ALU.subtract).then_inc(vst_ready, 1)
            v.wait_ge(w_ready, 1)
            for m, blk in ((1, WN), (2, WR)):
                last = nc.vector.tensor_scalar(LM[:, m, :, :], LM[:, 0, :, :], wsm[:, blk:blk + 1], None, ALU.mult)
            link(last)
            nc.vector.tensor_scalar(LM[:, 0, :, :], LM[:, 0, :, :], wsm[:, WM:WM + 1], None,
                                    ALU.mult).then_inc(lm_ready, 1)
            at = 0
            for t, (blk, n, quadrants) in enumerate(zip(OFFSET_BLOCKS, OFFSETS, OFFSET_QUADRANTS)):
                for q in quadrants:
                    if blk == WT:
                        last = nc.vector.tensor_copy(BL[:, t, :, q * Q:q * Q + n], bt[:, :, at:at + n])
                    else:
                        last = nc.vector.tensor_scalar(BL[:, t, :, q * Q:q * Q + n], bt[:, :, at:at + n],
                                                       wsm[:, blk:blk + 1], None, ALU.mult)
                last.then_inc(bl_ready, 1)
                at += n
            v.wait_ge(sel_in, 16 * 5)
            v.wait_ge(ulast_ready, 1)
            nc.vector.scalar_tensor_tensor(out=ub[:, :], in0=ULAST, scalar=ubc[:, 0:1], in1=ubc[:, 1:3],
                                           op0=ALU.add, op1=ALU.add)
            dec_low(4, 5)
            v.wait_ge(mlp_used, 4)
            link(nc.vector.tensor_tensor(vec, pM[0:C, :], svr[:, 1, :], ALU.add))
            link(nc.vector.bn_stats(vst[:, :], vec))
            link(nc.vector.bn_aggr(vmv[:, :], vst[:, :]))
            nc.vector.tensor_scalar(vrs[:, 0:1], vmv[:, 1:2], EPS, None, ALU.add).then_inc(var_ready, 1)
            dec_low(6)
            v.wait_ge(rst_ready, 1)
            link(nc.vector.tensor_scalar(vec, vec, vmv[:, 0:1], vrs[:, 2:3], ALU.subtract, ALU.mult))
            dec_low(7)
            link(nc.vector.tensor_tensor(vec, vec, svr[:, 2, :], ALU.mult))
            nc.vector.tensor_tensor(vec, vec, svr[:, 3, :], ALU.add).then_inc(vec_ready, 1)
            dec_low(8)
            dec_low(9, 10)
            v.wait_ge(vecT_sum, 1)
            v.wait_ge(lm_ready, 1)
            for m, blk in enumerate((WM, WN, WR)):
                for col in (RANK, 3 * Q + RANK):
                    last = nc.vector.tensor_scalar(LM[:, m, :, col:col + B],
                                                   VECT.rearrange("p (c j) -> p c j", j=C)[:, :, m * B:(m + 1) * B],
                                                   wsm[:, blk:blk + 1], None, ALU.mult)
            last.then_inc(lm_ready, 1)
            dec_low(11, 12)
            dec_low(13, 14, 15)
            fourth_bank(PAIRS - 1)
            v.wait_ge(u_in[KC - 1], 16 * B)
            v.wait_ge(u_in_act, 16 * B)
            features(nc.vector, KC - 1, link)

            def low_part(n, blk, src):
                v.wait_ge(w1_hi, n)
                nc.vector.scalar_tensor_tensor(out=W1[:, blk, LO, :, :], in0=block_of(src),
                                               scalar=wsm[:, src:src + 1], in1=W1[:, blk, HI, :, :].bitcast(F32),
                                               op0=ALU.mult, op1=ALU.subtract).then_inc(w1_lo, 1)

            wx = block_of(WM)

            def wx_add(n, blk):
                v.wait_ge(raw_in[blk], 16)
                if n == 0:
                    v.wait_ge(wx_m, 1)
                else:
                    v.wait_ge(wx_ready, n)
                nc.vector.scalar_tensor_tensor(out=wx, in0=block_of(blk), scalar=wsm[:, blk:blk + 1], in1=wx,
                                               op0=ALU.mult, op1=ALU.add).then_inc(wx_ready, 1)

            def after_first_inner():
                wx_add(0, WN)

            def after_first_stats():
                wx_add(1, WR)

            def after_first_embeddings():
                v.wait_ge(wx_hi, 1)
                nc.vector.tensor_tensor(W1[:, X, LO, :, :], wx, W1[:, X, HI, :, :].bitcast(F32),
                                        ALU.subtract).then_inc(wx_lo, 1)
                v.wait_ge(vw_ready, 1)
                link(nc.vector.tensor_copy(VWst[:, :], pVW[:, :]))
                nc.vector.tensor_tensor(VWst[3 * Q:P, :], pVW[3 * Q:P, :], VWst[3 * Q:P, :].bitcast(F32),
                                        ALU.subtract).then_inc(vwst_ready, 1)
                v.wait_ge(bt_sum, 1)
                link(nc.vector.tensor_copy(BT[:, :], pBT[:, :]))
                for q in (1, 3):
                    last = nc.vector.tensor_tensor(BT[q * Q:(q + 1) * Q, :], pBT[q * Q:(q + 1) * Q, :],
                                                   BT[q * Q:(q + 1) * Q, :].bitcast(F32), ALU.subtract)
                last.then_inc(bt_ready, 1)

            def split_w2():
                v.wait_ge(w2_hi, 1)
                nc.vector.tensor_tensor(W2[:, LO, :, :], w2raw[:, :, :], W2[:, HI, :, :].bitcast(F32),
                                        ALU.subtract).then_inc(w2_lo, 1)

            def split_lo(dst, hi, bank, have, t, done):
                v.wait_ge(have, t.count())
                nc.vector.tensor_tensor(dst.rearrange("p c t -> p (c t)"), bank[:, :],
                                        hi.bitcast(F32).rearrange("p c t -> p (c t)"), ALU.subtract).then_inc(done, 1)

            def stats(which, src, t, before, ready):
                nc.vector.bn_stats(bn[:, which, :], src).then_inc(bn_done, 1)
                parts[0] += 1
                v.wait_ge(bn_done, parts[0] if base[1] is None else base[1] * base[0] + parts[0])
                v.nop(nofuse=True)
                nc.vector.bn_aggr(mv[:, which, :], bn[:, which, :]).then_inc(ready, 1)

            parts = [0]
            base = [0, None]

            def h_stats(f):
                v.wait_ge(h1_ready, f.count())
                stats(1, h1[:, :], f, 0, mv2_ready)

            def h_norm(f):
                v.wait_ge(r2_ready, f.count())
                if f.plus(-1).exists():
                    v.wait_ge(hT, f.count(extra=0))
                nc.vector.tensor_scalar(ht[:, :], h1[:, :], mv[:, 1, 0:1], rs[:, 1:2],
                                        ALU.subtract, ALU.mult).then_inc(hn_ready, 1)

            def h_gain(f):
                v.wait_ge(hn_ready, f.count())
                nc.vector.tensor_tensor(ht[:, :], ht[:, :], ctt[:, f.slot, 0:D], ALU.mult).then_inc(h_ready, 1)

            def step(n):
                a, f, m, c = n.plus(2), n.plus(1), n, n.plus(-1)
                if f.exists():
                    s, bias = f.slot, ub[:, f.batch:f.batch + 1]
                    v.wait_ge(xu_ready, f.count())
                    nc.vector.tensor_scalar(inner[:, :], XU[:, 0:P], bias, None, ALU.add).then_inc(inner_part, 1)
                    v.wait_ge(inner_part, f.count())
                    nc.vector.tensor_tensor(inner[:, :], inner[:, :], XU[:, P:2 * P], ALU.add).then_inc(inner_ready, 1)
                    v.wait_ge(inner_ready, f.count())
                    if f.plus(-2).exists():
                        v.wait_ge(x_used, f.count(extra=-1))
                    nc.vector.tensor_copy(stack[:, s, :], inner[:, :]).then_inc(stack_part, 1)
                    v.wait_ge(stack_part, f.count())
                    nc.vector.tensor_tensor(stack[2 * Q:3 * Q, s, :], inner[2 * Q:3 * Q, :],
                                            stack[2 * Q:3 * Q, s, :].bitcast(F32), ALU.subtract) \
                        .then_inc(stack_ready, 1)
                if is_first(f):
                    after_first_inner()
                if m.exists():
                    split_lo(ops[:, 0, LO, :, :], ops[:, 0, HI, :, :], TP[0], t_hi, m, t_lo)
                    split_lo(ops[:, 1, LO, :, :], ops[:, 1, HI, :, :], TP[1], s_hi, m, s_lo)
                if is_first(m):
                    h_stats(m)
                    h_norm(m)
                    h_gain(m)
                    low_part(2, S_, WS)
                if a.exists():
                    s = a.slot
                    v.wait_ge(rep_in[s], a.slot_count(32))
                    if m.exists():
                        v.wait_ge(x_used, m.count())
                    nc.vector.tensor_scalar(OH[:, s, :], idxrep[:, s, :], inquad, None, ALU.is_equal).then_inc(oh_ready, 1)
                if f.exists():
                    s = f.slot
                    v.wait_ge(xv_ready, f.count())
                    v.wait_ge(x0_in[s], f.slot_count(16))
                    if f.plus(-2).exists():
                        v.wait_ge(xb_ready, f.count(extra=-1))
                    nc.vector.tensor_tensor(x1[:, s, :], XV[:, :], x0[:, s, :], ALU.add).then_inc(x1_ready, 1)
                if c.exists():
                    split_lo(zop[:, LO, :, :], zop[:, HI, :, :], TP[0], z_hi, c, z_lo)
                if is_first(m):
                    low_part(3, H, WH)
                    split_lo(ops[:, 2, LO, :, :], ops[:, 2, HI, :, :], TP[1], h_hi, m, h_lo)
                if f.exists():
                    v.wait_ge(x1_ready, f.count())
                    stats(0, x1[:, f.slot, :], f, 0, mv1_ready)
                if is_first(f):
                    after_first_stats()
                if f.exists():
                    s = f.slot
                    v.wait_ge(r1_ready, f.count())
                    if m.exists():
                        v.wait_ge(h1_part, m.count())
                    nc.vector.tensor_scalar(xhat[:, :], x1[:, s, :], mv[:, 0, 0:1], rs[:, 0:1],
                                            ALU.subtract, ALU.mult).then_inc(xhat_ready, 1)
                    v.wait_ge(xhat_ready, f.count())
                    v.wait_ge(ct_in[s], f.slot_count(16))
                    if m.exists():
                        v.wait_ge(tT, m.count())
                    nc.vector.tensor_tensor(tt[:, :], xhat[:, :], ctt[:, s, D:2 * D], ALU.mult).then_inc(t_ready, 1)
                    v.wait_ge(sg_in[s], f.slot_count(16))
                    if m.exists():
                        v.wait_ge(sT, m.count())
                    nc.vector.tensor_tensor(st[:, :], xhat[:, :], sgt[:, s, :], ALU.mult).then_inc(s_ready, 1)
                if is_first(f):
                    after_first_embeddings()
                if is_first(m):
                    split_w2()
                if m.exists() and not is_first(m):
                    split_lo(ops[:, 2, LO, :, :], ops[:, 2, HI, :, :], TP[1], h_hi, m, h_lo)
                if f.exists() and not is_first(f):
                    h_stats(f)
                if c.exists():
                    if is_first(c):
                        v.wait_ge(rows_in, 32)
                    v.wait_ge(w2_done, c.count())
                    nc.vector.tensor_tensor(o[:, :], OUT[c.slot][:, :], b2bc[:, :], ALU.add).then_inc(o_ready, 1)
                    v.wait_ge(o_ready, c.count())
                    stats(2, o[:, :], c, 0, mv3_ready)
                if f.exists() and not is_first(f):
                    h_norm(f)
                if c.exists():
                    v.wait_ge(mv3_ready, c.count())
                    nc.vector.scalar_tensor_tensor(out=u[:, :], in0=o[:, :], scalar=mv[:, 2, 0:1], in1=gbc[:, :],
                                                   op0=ALU.subtract, op1=ALU.mult).then_inc(u_ready, 1)
                if f.exists() and not is_first(f):
                    h_gain(f)
                if c.exists():
                    s = c.slot
                    v.wait_ge(u_ready, c.count())
                    v.wait_ge(r3_ready, c.count())
                    v.wait_ge(xb_ready, c.count())
                    if c.plus(-2).exists():
                        v.wait_ge(stored[s], c.plus(-2).slot_count(16))
                    nc.vector.scalar_tensor_tensor(out=y[:, s, :], in0=u[:, :], scalar=rs[:, 2:3], in1=xb[:, s, :],
                                                   op0=ALU.mult, op1=ALU.add).then_inc(y_ready, 1)

            for n in range(-2, FIRST):
                step(Tile(n))
            with v.Fori(0, (LAST - FIRST) // 2) as i:
                before = parts[0]
                base[:] = [6, i]
                step(Tile(FIRST, i))
                step(Tile(FIRST + 1, i))
                assert parts[0] - before == 6
            parts[0] = before + 6 * ((LAST - FIRST) // 2)
            base[1] = None
            for n in range(LAST, TILES + 1):
                step(Tile(n))


def kernel(**inputs):
    import concourse.bacc as bacc
    from concourse.bass_utils import run_bass_kernel_spmd

    a = {n: np.asarray(v) for n, v in inputs.items()}

    def tiled(v):
        return v.reshape(B, S // P, P, *v.shape[2:])

    def put(rows, cols, *parts):
        r = np.zeros((rows, cols), np.float32)
        for i, j, v in parts:
            r[i:i + v.shape[0], j:j + v.shape[1]] = v
        return r

    def chunks(v):
        return v.reshape(-1, P, v.shape[-1]).transpose(1, 0, 2)

    x = tiled(a["x"])
    V, W_dec, b_dec = a["L0_cond_V"], a["L0_cond_W_dec"], a["L0_cond_b_dec"]
    L1 = {n[len("L1_cond_"):]: v for n, v in a.items() if n.startswith("L1_cond_")}
    path, comp, scale = (tiled(a[n]) for n in ("itok_BxS_0_999", "itok_BxS_0_4", "mask_BxS_ik0"))
    NDEC = D * RANK
    consts = put(P, P + 1, (0, 0, np.eye(P, dtype=np.float32)),
                 (0, P, (np.arange(P) % Q).astype(np.float32)[:, None]))
    batch_eye = np.eye(B, dtype=np.float32)
    spare = (RANK, 3 * Q + RANK)
    mlps = ("mem", "noi", "res")
    arrays = {
        "x": x,
        "xT": x.reshape(B, S // P, P, KC, P).transpose(0, 1, 4, 3, 2),
        "idx": np.stack([path, comp, scale], axis=-1),
        "rows": np.stack([comp, scale], axis=1),
        "consts": consts,
        "ubc": put(P, 3, *[(q * Q, 0, b_dec[NDEC:, None]) for q in (0, 2, 3)], *[(r, 1, batch_eye) for r in spare]),
        "selrow": put(1, P, *[(0, r, np.ones((1, B), np.float32)) for r in spare]),
        "int_b1": L1["int_b1"][None], "int_b2": L1["int_b2"][None], "int_g": L1["int_g"][None],
        "int_be": L1["int_be"][None], "aw": L1["aw"][None],
        "cond": chunks(put(2 * MU, C, (0, 0, a["cond_512"].T), (MU, B, a["cond_64"].T),
                           (MU + P, 2 * B, a["fside_Bx32_0"].T))),
        "mlp_W1": chunks(put(2 * MU, D, (0, 0, L1["mem_W1"]), (MU, 0, L1["noi_W1"]), (MU + P, 0, L1["res_W1"]))),
        "svr": np.stack([np.repeat(np.stack([L1[f"{m}_{w}"] for m in mlps]), B, axis=0)
                         for w in ("b1", "b2", "g", "be")], axis=1),
        "bdec": b_dec[:NDEC].reshape(D, RANK),
        "wlast": put(MU, P, *[(0, q * Q, W_dec[:, NDEC:]) for q in (0, 2, 3)]),
        "W_dec": W_dec,
        "VT4": put(D, P, *[(0, q * Q, V.T) for q in range(4)]).reshape(KC, P, P).transpose(1, 0, 2),
        "V4": put(P, D, *[(q * Q, 0, V) for q in range(4)]),
        "bt": chunks(np.concatenate([L1["tm_b"].T, L1["ms_b"].T, L1["cp_b"].T], axis=1)),
        "pw": np.concatenate([L1["pw_g"], L1["pw_b"]], axis=1),
        "ct": np.concatenate([L1["cp_g"], L1["tm_g"]], axis=1),
        "ms_g": L1["ms_g"],
        "int_W1": L1["int_W1"], "int_W2": L1["int_W2"],
    }
    arrays.update({f"{m}_W2": L1[f"{m}_W2"] for m in mlps})
    arrays = {n: np.ascontiguousarray(v) for n, v in arrays.items()}

    nc = bacc.Bacc("TRN2", target_bir_lowering=False, num_devices=1)
    d = {n: nc.dram_tensor("in_" + n, v.shape, mybir.dt.from_np(v.dtype), kind="ExternalInput").ap()
         for n, v in arrays.items()}
    out = nc.dram_tensor("out", (B, S, D), F32, kind="ExternalOutput").ap()
    build(nc, d, out)
    return run_bass_kernel_spmd(nc, [{"in_" + n: v for n, v in arrays.items()}], core_ids=[0]).results[0]["out"]
```
